# Optimizing a Trainium2 kernel written in Bass

```python
import numpy as np
import jax
import jax.numpy as jnp

def _softmax(x, axis=-1):
    return jax.nn.softmax(x, axis=axis)

def _gelu(x):
    return jax.nn.gelu(x, approximate=True)

def _silu(x):
    return jax.nn.silu(x)

def _sigmoid(x):
    return jax.nn.sigmoid(x)

def _layernorm(x, axis=-1, eps=1e-05):
    m = jnp.mean(x, axis=axis, keepdims=True)
    v = jnp.var(x, axis=axis, keepdims=True)
    return (x - m) / jnp.sqrt(v + eps)

def _scatter_add(tgt, idx, src, axis=0):
    return tgt.at[idx].add(src)

def _segment_sum(src, seg, n):
    return jax.ops.segment_sum(src, seg, n)
kernel_name = 'mk_xattn_ffn_d1_seqx_r4_b46b9a'

def setup_inputs(seed: int=0):
    np.random.seed(seed)
    _w = jnp.asarray

    def _rec_inputs():
        import jax
        import jax.numpy as jnp
        _rk = jax.random.key(seed)
        x = 7.22e-05 + 1 * jax.random.normal(jax.random.fold_in(_rk, 1), (32, 128, 512), jnp.float32)
        _lenS = 128 - jax.random.randint(jax.random.fold_in(_rk, 7), (32,), 0, max(1, 128 // 4) + 1, jnp.int32)
        _lenS2 = 128 - jax.random.randint(jax.random.fold_in(_rk, 8), (32,), 0, max(1, 128 // 4) + 1, jnp.int32)
        _ctx_512P = jax.random.normal(jax.random.fold_in(_rk, 11), (32, 16, 128), jnp.float32)
        _ctx_512c = jax.random.dirichlet(jax.random.fold_in(_rk, 511), 0.3 * jnp.ones((16,), jnp.float32), (32, 128))
        _ctx_512t = jnp.einsum('bsk,bkd->bsd', _ctx_512c, _ctx_512P)
        _ctx_512t = _ctx_512t * jax.lax.rsqrt(jnp.mean(jnp.square(_ctx_512t)) + 1e-12) * 0.953939
        ctx_512 = -0.000514642 + 1.00011 * (_ctx_512t + 0.3 * jax.random.normal(jax.random.fold_in(_rk, 611), (32, 128, 128), jnp.float32))
        return (x, ctx_512)
    x, ctx_512 = _rec_inputs()

    def _L0_xattn_setup():
        import jax, jax.numpy as jnp
        import numpy as np
        N_HEADS = 16
        N_KV_HEADS = 4
        ROPE_THETA = 10000.0
        EPS = 1e-05

        def _rms_norm(x, w):
            var = jnp.mean(x * x, axis=-1, keepdims=True)
            return x * jax.lax.rsqrt(var + EPS) * w

        def _rope_sin_cos(T, head_dim, dtype):
            inv_freq = 1.0 / ROPE_THETA ** (jnp.arange(0, head_dim, 2, dtype=jnp.float32) / head_dim)
            t = jnp.arange(T, dtype=jnp.float32)
            freqs = jnp.outer(t, inv_freq)
            emb = jnp.concatenate([freqs, freqs], -1)
            return (jnp.sin(emb).astype(dtype)[None, None], jnp.cos(emb).astype(dtype)[None, None])

        def _rotate_half(x):
            h = x.shape[-1] // 2
            x1, x2 = (x[..., :h], x[..., h:])
            return jnp.concatenate([-x2, x1], axis=-1)
        key = jax.random.key(seed)
        ks = jax.random.split(key, 6)
        B, T, C = (2, 512, 512)
        Ckv = C // N_HEADS * N_KV_HEADS
        return {'q': jax.random.normal(ks[0], (B, T, C), jnp.float32), 'k': jax.random.normal(ks[1], (B, T, Ckv), jnp.float32), 'v': jax.random.normal(ks[2], (B, T, Ckv), jnp.float32), 'q_norm_w': jnp.ones((C,), jnp.float32), 'k_norm_w': jnp.ones((Ckv,), jnp.float32), 'w_out': jax.random.normal(ks[3], (C, C), jnp.float32) * C ** (-0.5)}
    _L0_xattn_all = _L0_xattn_setup()
    _L0_xattn_in = {k: v for k, v in _L0_xattn_all.items() if k in ('q_norm_w', 'k_norm_w', 'w_out')}
    del _L0_xattn_all

    def _L0_ffn_setup():
        import jax, jax.numpy as jnp
        import numpy as np
        _FP8_MAX = 448.0
        _BLOCK = 32
        _EPS = 1e-30

        def _mx_dequant(t):
            rows, feat = t.shape
            blocks = t.reshape(rows, feat // _BLOCK, _BLOCK)
            max_abs = jnp.max(jnp.abs(blocks), axis=-1)
            scales = jnp.maximum(max_abs / _FP8_MAX, _EPS)
            q = (blocks / scales[..., None]).astype(jnp.float8_e4m3fn).astype(jnp.float32)
            return (q * scales[..., None]).reshape(rows, feat)

        def _mx_linear(x2d, w):
            return _mx_dequant(x2d) @ _mx_dequant(w).T
        key = jax.random.key(seed)
        k1, k2, k3, k4 = jax.random.split(key, 4)
        B, S, H, I = (2, 256, 512, 2048)
        return {'x': jax.random.normal(k1, (B, S, H), dtype=jnp.float32), 'gate_w': jax.random.normal(k2, (I, H), dtype=jnp.float32) * 0.02, 'up_w': jax.random.normal(k3, (I, H), dtype=jnp.float32) * 0.02, 'down_w': jax.random.normal(k4, (H, I), dtype=jnp.float32) * 0.02}
    _L0_ffn_all = _L0_ffn_setup()
    _L0_ffn_in = {k: v for k, v in _L0_ffn_all.items() if k in ('gate_w', 'up_w', 'down_w')}
    del _L0_ffn_all
    return {'x': x, 'ctx_512': ctx_512, 'L0_xattn_q_norm_w': _L0_xattn_in['q_norm_w'], 'L0_xattn_k_norm_w': _L0_xattn_in['k_norm_w'], 'L0_xattn_w_out': _L0_xattn_in['w_out'], 'L0_ffn_gate_w': _L0_ffn_in['gate_w'], 'L0_ffn_up_w': _L0_ffn_in['up_w'], 'L0_ffn_down_w': _L0_ffn_in['down_w']}

def reference(x, ctx_512, L0_xattn_q_norm_w, L0_xattn_k_norm_w, L0_xattn_w_out, L0_ffn_gate_w, L0_ffn_up_w, L0_ffn_down_w):
    import jax
    import jax.numpy as jnp

    def _L0_xattn_ref(q, k, v, q_norm_w, k_norm_w, w_out):
        import jax, jax.numpy as jnp
        import numpy as np
        N_HEADS = 16
        N_KV_HEADS = 4
        ROPE_THETA = 10000.0
        EPS = 1e-05

        def _rms_norm(x, w):
            var = jnp.mean(x * x, axis=-1, keepdims=True)
            return x * jax.lax.rsqrt(var + EPS) * w

        def _rope_sin_cos(T, head_dim, dtype):
            inv_freq = 1.0 / ROPE_THETA ** (jnp.arange(0, head_dim, 2, dtype=jnp.float32) / head_dim)
            t = jnp.arange(T, dtype=jnp.float32)
            freqs = jnp.outer(t, inv_freq)
            emb = jnp.concatenate([freqs, freqs], -1)
            return (jnp.sin(emb).astype(dtype)[None, None], jnp.cos(emb).astype(dtype)[None, None])

        def _rotate_half(x):
            h = x.shape[-1] // 2
            x1, x2 = (x[..., :h], x[..., h:])
            return jnp.concatenate([-x2, x1], axis=-1)
        B, T, C = q.shape
        hd = C // N_HEADS
        g = N_HEADS // N_KV_HEADS
        q = _rms_norm(q, q_norm_w)
        k = _rms_norm(k, k_norm_w)
        q = q.reshape(B, T, N_HEADS, hd).transpose(0, 2, 1, 3)
        k = k.reshape(B, T, N_KV_HEADS, hd).transpose(0, 2, 1, 3)
        v = v.reshape(B, T, N_KV_HEADS, hd).transpose(0, 2, 1, 3)
        sin, cos = _rope_sin_cos(T, hd, q.dtype)
        q = q * cos + _rotate_half(q) * sin
        k = k * cos + _rotate_half(k) * sin
        qg = q.reshape(B, N_KV_HEADS, g, T, hd)
        scale = 1.0 / jnp.sqrt(jnp.asarray(hd, q.dtype))
        scores = jnp.einsum('bgnqd,bgkd->bgnqk', qg, k) * scale
        causal = jnp.tril(jnp.ones((T, T), bool))
        scores = jnp.where(causal, scores, jnp.asarray(-1e+30, scores.dtype))
        attn = jax.nn.softmax(scores, axis=-1)
        out = jnp.einsum('bgnqk,bgkd->bgnqd', attn, v)
        out = out.reshape(B, N_HEADS, T, hd).transpose(0, 2, 1, 3).reshape(B, T, C)
        return out @ w_out.T

    def _L0_ffn_ref(x, gate_w, up_w, down_w):
        import jax, jax.numpy as jnp
        import numpy as np
        _FP8_MAX = 448.0
        _BLOCK = 32
        _EPS = 1e-30

        def _mx_dequant(t):
            rows, feat = t.shape
            blocks = t.reshape(rows, feat // _BLOCK, _BLOCK)
            max_abs = jnp.max(jnp.abs(blocks), axis=-1)
            scales = jnp.maximum(max_abs / _FP8_MAX, _EPS)
            q = (blocks / scales[..., None]).astype(jnp.float8_e4m3fn).astype(jnp.float32)
            return (q * scales[..., None]).reshape(rows, feat)

        def _mx_linear(x2d, w):
            return _mx_dequant(x2d) @ _mx_dequant(w).T
        B, S, H = x.shape
        x2d = x.reshape(B * S, H)
        gate = _mx_linear(x2d, gate_w)
        up = _mx_linear(x2d, up_w)
        h = jax.nn.silu(gate) * up
        out = _mx_linear(h, down_w)
        return out.reshape(B, S, H)
    x = x + _L0_xattn_ref(_layernorm(x, axis=-1), ctx_512, ctx_512, L0_xattn_q_norm_w, L0_xattn_k_norm_w, L0_xattn_w_out)
    x = x + _L0_ffn_ref(_layernorm(x, axis=-1), L0_ffn_gate_w, L0_ffn_up_w, L0_ffn_down_w)
    return x

_drawn_inputs = setup_inputs


def setup_inputs(seed=0):
    import zlib

    import numpy as np

    out = dict(_drawn_inputs(seed))
    spreads = {'L0_xattn_q_norm_w': (1.0, 0.2), 'L0_xattn_k_norm_w': (1.0, 0.2)}
    factors = {}
    for name, (base, spread) in spreads.items():
        noise = np.random.default_rng([zlib.crc32(name.encode()), seed]).standard_normal(out[name].shape)
        drawn = base * np.exp(spread * noise) if base else spread * noise
        out[name] = jnp.asarray(drawn.astype(out[name].dtype))
    for name, factor in factors.items():
        out[name] = (out[name] * factor).astype(out[name].dtype)
    return out
```

```python
from contextlib import ExitStack

import concourse.bass as bass
from concourse import mybir


P = 128
ALU = mybir.AluOpType
ACT = mybir.ActivationFunctionType
AX = mybir.AxisListType.X
F32 = mybir.dt.float32
F16 = mybir.dt.float16
U32 = mybir.dt.uint32
RMAX = bass.bass_isa.ReduceOp.max

EPS = 1e-5
FP8_MAX = 448.0
SCALE_FLOOR = 1e-30
BLOCK = 32
MIN_NORMAL = 2.0 ** -6
MAGIC = 1.5 * 2.0 ** 20
EXPONENT = 0x7F800000
MASKED = -1e30

HD = 32
LEAD = 20
GROUP = 8


def bass_xattn_ffn(nc, x, ctx_in, q_norm_w, k_norm_w, w_out, gate_w, up_w, down_w,
                   rope_cos, rope_sin, causal, eye32, eye16, out):
    B, T, C = x.shape
    CK = ctx_in.shape[2]
    I = gate_w.shape[0]
    NH, NK = C // HD, CK // HD
    NR = NH // NK
    NQK = NH + NK
    KT = C // P
    IT = I // P
    NB = C // BLOCK
    GT = 2 * P
    STEPS = B * NK
    assert T == P and IT == 2 * GROUP and NK == 4 and CK == P and C == 512 and STEPS % GROUP == 0
    KD = HD + 1
    TILES = IT

    x_rows = x.rearrange("b t c -> (b t) c")
    ctx_rows = ctx_in.rearrange("b t c -> (b t) c")
    out_rows = out.rearrange("b t c -> (b t) c")
    x1_rows = nc.dram_tensor("x1_scratch", (B * T, C), F32, kind="Internal").ap()
    xq_rows = nc.dram_tensor("xq_scratch", (B * P, KT * P), F32, kind="Internal").ap()

    with ExitStack() as stack:
        def sb(name, shape, dt):
            return stack.enter_context(nc.sbuf_tensor(name, shape, dt))

        def bank(name):
            return stack.enter_context(nc.psum_tensor(name, [P, 512], F32))

        def sem(name):
            return stack.enter_context(nc.semaphore(name))

        gate_t = sb("gate_t", [P, 2, KT, I], F16)
        up_t = sb("up_t", [P, 2, KT, I], F16)
        down_t = sb("down_t", [P, 2, IT, C], F16)
        wo_t = sb("wo_t", [P, 2, KT, C], F16)
        rope_c = sb("rope_c", [P, NQK, HD], F32)
        rope_s = sb("rope_s", [P, NQK, HD], F32)
        mask = sb("mask", [P, P], F32)
        ident = sb("ident", [P, P], F32)
        ident16 = sb("ident16", [P, P], F16)
        cos_sb = sb("cos_sb", [P, HD], F32)
        sin_sb = sb("sin_sb", [P, HD], F32)
        half_neg = sb("half_neg", [P, 2], F32)
        peak = sb("peak", [P, 8], F32)
        pow2 = sb("pow2", [P, 8], F32)
        inv2 = sb("inv2", [P, 8], F32)
        fac = sb("fac", [P, 12], F32)
        PQ, PK, PC, PG, PU, PD, PO = range(7)
        FQ, FK, FS, FV, FW, FO, FTH, FFL, FWO, FTMP = (fac[:, n:n + 1] for n in range(10))

        AREA = 24832
        area = sb("area", [P, AREA], F32)
        taken = [0]

        def carve(words):
            at = taken[0]
            taken[0] += words
            assert taken[0] <= AREA, taken[0]
            return area[:, at:at + words]

        def carve16(count):
            return carve(count // 2).bitcast(F16)

        xs = carve(KT * GT).rearrange("p (m k t) -> p m k t", m=2, k=KT)
        xh = carve16(KT * GT).rearrange("p (m k t) -> p m k t", m=2, k=KT)
        xl = carve16(KT * GT).rearrange("p (m k t) -> p m k t", m=2, k=KT)
        th = carve(512)
        hh32 = carve(512)
        yq = [carve(512) for _ in range(2)]
        em = carve(512)
        sbc = [carve(1024).rearrange("p (w n) -> p w n", w=2) for _ in range(2)]
        hd = carve(512)
        hpart = [carve16(1024).rearrange("p (w n) -> p w n", w=2) for _ in range(2)]
        x1f = [carve(C) for _ in range(2)]
        yout = [carve(C) for _ in range(2)]
        hmax = carve(16)
        hsc = carve(32)
        xt = [carve(C) for _ in range(2)]
        ct = [carve(CK) for _ in range(2)]
        xn = carve(NQK * HD).rearrange("p (h d) -> p h d", d=HD)
        qc = carve(NQK * HD).rearrange("p (h d) -> p h d", d=HD)
        qs = carve(NQK * HD).rearrange("p (h d) -> p h d", d=HD)
        parts = [carve16(NQK * 4 * HD).rearrange("p (h w d) -> p h w d", w=4, d=HD) for _ in range(2)]
        vpart = [[carve16(136)[:, 0:NK * KD].rearrange("p (g d) -> p g d", d=KD) for _ in range(2)]
                 for _ in range(2)]
        qkt = [carve16((NR + 1) * P).rearrange("p (h t) -> p h t", t=P) for _ in range(2)]
        sm = [carve(NR * P).rearrange("p (h t) -> p h t", t=P) for _ in range(2)]
        nmax = [carve(NR) for _ in range(2)]
        pt = [[carve16(NR * P).rearrange("p (h t) -> p h t", t=P) for _ in range(2)] for _ in range(2)]
        rsum = carve(NR)
        ao = [carve(C) for _ in range(2)]
        aot = [carve16(C).rearrange("p (k t) -> p k t", t=P) for _ in range(2)]
        xr = [carve(C) for _ in range(2)]
        x1 = [carve(C) for _ in range(2)]
        xn2 = carve(C)
        xy = carve(C)
        xem = carve(C)
        xsc = carve(3 * NB)
        xqt = carve(C)
        bst = carve(8)
        mv = carve(4)
        cbst = carve(8)
        cmv = carve(4)
        arg = carve(2)
        rstd = carve(2)
        bst2 = carve(8)
        mv2 = carve(4)
        arg2 = carve(2)
        rstd2 = carve(2)

        raws = [area[:, n * 8192:(n + 1) * 8192].rearrange("p (n k) -> p n k", k=512) for n in range(2)]
        wy = [area[:, 16384 + n * 512:16384 + (n + 1) * 512] for n in range(2)]
        wem = area[:, 17408:17920]
        wd = [area[:, 17920 + n * 512:17920 + (n + 1) * 512] for n in range(2)]
        wblk = area[:, 19456:19456 + 3 * 256].rearrange("p (w n) -> p w n", w=3)
        norm_b = area[:, 20480:20480 + NQK * HD].rearrange("p (h d) -> p h d", d=HD)

        bk_acc = [bank("bk_acc0"), bank("bk_acc1")]
        bk_gate = bank("bk_gate")
        bk_up = bank("bk_up")
        bk_qo = bank("bk_qo")
        bk_s = bank("bk_s")
        bk_pt = bank("bk_pt")
        bk_row = bank("bk_row")
        qk_ps = bk_qo[:, 0:(NR + 1) * P // 2].bitcast(F16).rearrange("p (h t) -> p h t", t=P)
        o_ps = bk_qo[:, 352:352 + NR * 36].rearrange("p (h d) -> p h d", d=36)

        consts_in = sem("consts_in")
        norm_in = sem("norm_in")
        ctx_all_in = sem("ctx_all_in")
        raw_in = [sem(f"raw_in{n}") for n in range(4)]
        su = sem("su")
        su_peak = sem("su_peak")
        su_gmax = sem("su_gmax")
        su_pool = sem("su_pool")
        w_scale = sem("w_scale")
        w_y = sem("w_y")
        w_q = sem("w_q")
        w_d = sem("w_d")
        w_t = sem("w_t")
        w_hi = sem("w_hi")
        w_lo = sem("w_lo")
        fwo_ready = sem("fwo_ready")
        sp_waited = sem("sp_waited")
        v_waited = sem("v_waited")
        setup_done = sem("setup_done")

        x_in = [sem("x_in0"), sem("x_in1")]
        xr_in = [sem("xr_in0"), sem("xr_in1")]
        st1 = sem("st1")
        arg_ready = sem("arg_ready")
        rstd_ready = sem("rstd_ready")
        xn_ready = sem("xn_ready")
        qcs_ready = sem("qcs_ready")
        qr_ready = sem("qr_ready")
        qhi_ready = sem("qhi_ready")
        qlo_ready = sem("qlo_ready")
        stack_ready = sem("stack_ready")
        vhi_ready = sem("vhi_ready")
        v_ready = sem("v_ready")
        t_ready = sem("t_ready")
        qkt_ready = sem("qkt_ready")
        s_ready = sem("s_ready")
        sm_ready = sem("sm_ready")
        nmax_ready = sem("nmax_ready")
        p_ready = sem("p_ready")
        pt_ready = sem("pt_ready")
        ph_ready = sem("ph_ready")
        pl_ready = sem("pl_ready")
        o_ready = sem("o_ready")
        rsum_ready = sem("rsum_ready")
        ao_ready = sem("ao_ready")
        aot_ready = sem("aot_ready")
        aoh_ready = sem("aoh_ready")
        aol_ready = sem("aol_ready")
        w_ready = sem("w_ready")
        x1_ready = sem("x1_ready")
        st2 = sem("st2")
        arg2_ready = sem("arg2_ready")
        rstd2_ready = sem("rstd2_ready")
        xn2_ready = sem("xn2_ready")
        xst = sem("xst")
        xsc_ready = sem("xsc_ready")
        xy_ready = sem("xy_ready")
        xeq = sem("xeq")
        xqq_ready = sem("xqq_ready")
        xd_ready = sem("xd_ready")
        xdt_ready = sem("xdt_ready")
        xqt_ready = sem("xqt_ready")
        x1_out = [sem("x1_out0"), sem("x1_out1")]
        xq_out = [sem("xq_out0"), sem("xq_out1")]

        xs_in = sem("xs_in")
        x1f_in = sem("x1f_in")
        xh_ready = sem("xh_ready")
        xl_ready = sem("xl_ready")
        g_ready = sem("g_ready")
        u_ready = sem("u_ready")
        th_ready = sem("th_ready")
        ga_ready = sem("ga_ready")
        h_ready = sem("h_ready")
        hst = sem("hst")
        sbc_ready = sem("sbc_ready")
        y_ready = sem("y_ready")
        heq = sem("heq")
        q_ready = sem("q_ready")
        hd_ready = sem("hd_ready")
        hhi_ready = sem("hhi_ready")
        hlo_ready = sem("hlo_ready")
        d_done = sem("d_done")
        acc_ready = sem("acc_ready")
        yout_ready = sem("yout_ready")
        y_out = [sem("y_out0"), sem("y_out1")]

        block = stack.enter_context(nc.Block())

        def ge(eng, s, value):
            if not isinstance(value, int) or value > 0:
                eng.wait_ge(s, value)

        def ffn_live(b, c):
            return not isinstance(b, int) or 0 <= b + c < STEPS

        def unit_live(b, c):
            return not isinstance(b, int) or 0 <= b + c + LEAD < STEPS

        def drive(eng, body):
            first = -3 * GROUP
            lo, hi = GROUP, STEPS - 3 * GROUP
            for b in range(first, lo, GROUP):
                body(b)
            with eng.Fori(lo // GROUP, hi // GROUP) as group:
                body(eng.snap(group * GROUP))
            for b in range(hi, STEPS + GROUP, GROUP):
                body(b)

        def dma_count(b, four_t):
            return b * 2 + 2 * four_t - 8 * ((four_t // 4) % 2) + 16

        def rot(ap):
            return ap.rearrange("p h (two e) -> p h two e", two=2)[:, :, ::-1, :]

        def halves(ap):
            return ap.rearrange("p h (two e) -> p h two e", two=2)

        def blocks(ap):
            return ap.rearrange("p (n k) -> p n k", k=BLOCK)

        def spread(ap, n):
            return ap.unsqueeze(2).broadcast_to([P, n, BLOCK])

        def weight_slot(t):
            w, n = divmod(t, TILES)
            if w < 2:
                dst = (gate_t, up_t)[w]
                return (lambda part: dst[:, part, :, n * P:(n + 1) * P]), 1.0
            if w == 2:
                rt, cc = divmod(n, 4)
                return (lambda part: down_t[:, part, 4 * cc:4 * cc + 4, rt * P:(rt + 1) * P]), 1.0
            return (lambda part: wo_t[:, part, :, n * P:(n + 1) * P]), FWO

        @block.sync
        def _(sp):
            sp.dma_start(norm_b[:, 0:NH, :].rearrange("p h d -> p (h d)"),
                         q_norm_w.rearrange("(a n) -> a n", a=1).broadcast_to([P, C])).then_inc(norm_in, 16)
            sp.dma_start(norm_b[:, NH:NQK, :].rearrange("p h d -> p (h d)"),
                         k_norm_w.rearrange("(a n) -> a n", a=1).broadcast_to([P, CK])).then_inc(norm_in, 16)
            for dst, src in ((mask, causal), (ident, eye32), (ident16, eye16), (cos_sb, rope_cos), (sin_sb, rope_sin)):
                sp.dma_start(dst[:], src).then_inc(consts_in, 16)
            sp.dma_start(raws[1][:, 0:B * CK // 512, :].rearrange("p n (b c) -> p (n b) c", c=CK),
                         ctx_in.rearrange("b t c -> t b c")).then_inc(ctx_all_in, 16)
            row_major = "(n p) k -> p n k"
            sp.dma_start(raws[0][:], gate_w.rearrange(row_major, p=P)).then_inc(raw_in[0], 16)
            sp.wait_ge(su_peak, 3)
            sp.dma_start(raws[1][:], up_w.rearrange(row_major, p=P)).then_inc(raw_in[1], 16)
            sp.wait_ge(w_y, TILES)
            sp.dma_start(raws[0].rearrange("p (n q) k -> p n (q k)", q=4),
                         down_w.rearrange(row_major, p=P)).then_inc(raw_in[2], 16)
            sp.wait_ge(w_y, 2 * TILES)
            sp.dma_start(raws[1][:, 0:KT, :], w_out.rearrange(row_major, p=P)).then_inc(raw_in[3], 16)
            sp.wait_ge(setup_done, 1)

            def tile_rows(b, k_const, p):
                return b * 32 + (k_const - p) * 32

            def body(b):
                live = not isinstance(b, int)
                for c in range(GROUP):
                    kc = c + LEAD

                    def tile_live(p):
                        return (kc - p) % 4 == 0 and (live or 0 <= b + kc - p < STEPS)

                    if tile_live(-4):
                        par = ((kc + 4) // 4) % 2
                        at = sp.snap(tile_rows(b, kc, -4)) if live else tile_rows(b, kc, -4)
                        ge(sp, qcs_ready, b + kc + 4 - 4)
                        ge(sp, v_ready, b + kc + 4 - 4)
                        sp.dma_start(xt[par], x_rows[bass.ds(at, P), :]).then_inc(x_in[par], 16)
                        sp.dma_start(ct[par], ctx_rows[bass.ds(at, P), :]).then_inc(x_in[par], 16)
                    if tile_live(5):
                        par = ((kc - 5) // 4) % 2
                        at = sp.snap(tile_rows(b, kc, 5)) if live else tile_rows(b, kc, 5)
                        ge(sp, x1_ready, b + kc - 5 - 4)
                        sp.dma_start(xr[par], x_rows[bass.ds(at, P), :]).then_inc(xr_in[par], 16)
                    if tile_live(9):
                        par = ((kc - 9) // 4) % 2
                        at = sp.snap(tile_rows(b, kc, 9)) if live else tile_rows(b, kc, 9)
                        ge(sp, x1_ready, b + kc - 9 + 4)
                        sp.dma_start(x1_rows[bass.ds(at, P), :], x1[par]).then_inc(x1_out[par], 16)
                    if tile_live(14):
                        par = ((kc - 14) // 4) % 2
                        at = sp.snap(tile_rows(b, kc, 14)) if live else tile_rows(b, kc, 14)
                        ge(sp, xqt_ready, b + kc - 14 + 4)
                        sp.dma_start(xq_rows[bass.ds(at, P), :], xqt).then_inc(xq_out[par], 16)
                    if c == 6 and (live or 0 <= b + GROUP < STEPS):
                        at = sp.snap(b * 32 + GROUP * 32) if live else (b + GROUP) * 32
                        for par in range(2):
                            ge(sp, xq_out[par], b * 2 + 32)
                        sp.sem_inc(sp_waited, 1)
                        ge(sp, xl_ready, b + GROUP)
                        sp.dma_start(xs, xq_rows[bass.ds(at, GT), :].rearrange("(m p) (k t) -> p m k t", m=2, k=KT)
                                     ).then_inc(xs_in, 16)
                    if c == 3 and (live or 0 <= b < STEPS):
                        for m in range(2):
                            at = sp.snap(b * 32 + m * P) if live else b * 32 + m * P
                            ge(sp, x1_out[m], b * 2 + 16)
                            ge(sp, y_out[m], b * 2)
                            sp.dma_start(x1f[m], x1_rows[bass.ds(at, P), :]).then_inc(x1f_in, 16)
                    if c == 2 and (live or 0 <= b - GROUP < STEPS):
                        for m in range(2):
                            at = sp.snap(b * 32 + (m * P - GROUP * 32)) if live else (b - GROUP) * 32 + m * P
                            ge(sp, yout_ready, b - 4 + 4 * m)
                            sp.dma_start(out_rows[bass.ds(at, P), :], yout[m]).then_inc(y_out[m], 16)

            drive(sp, body)
            for m in range(2):
                sp.wait_ge(y_out[m], 16 * STEPS // GROUP)
                sp.wait_ge(x1_out[m], 16 * STEPS // GROUP)
                sp.wait_ge(xq_out[m], 16 * STEPS // GROUP)

        @block.tensor
        def _(pe):
            pe.wait_ge(consts_in, 80)
            for t in range(3 * TILES + KT):
                if t < 3 * TILES:
                    pe.wait_ge(w_d, t + 1)
                    src = wd[t % 2]
                else:
                    pe.wait_ge(su_gmax, 5)
                    src = raws[1][:, t - 3 * TILES, :]
                if t >= 2:
                    pe.wait_ge(w_lo, t - 1)
                for n in range(4):
                    last = pe.transpose((bk_pt if t % 2 else bk_row)[:, n * P:(n + 1) * P],
                                        src[:, n * P:(n + 1) * P], ident[:])
                last.then_inc(w_t, 1)

            def three(dst, lhs_hi, lhs_lo, rhs_hi, rhs_lo, start, stop):
                pe.matmul(dst, lhs_hi, rhs_hi, start=start, stop=False)
                pe.matmul(dst, lhs_hi, rhs_lo, start=False, stop=False)
                return pe.matmul(dst, lhs_lo, rhs_hi, start=False, stop=stop)

            def body(b):
                live = not isinstance(b, int)
                for c in range(GROUP):
                    kc = c + LEAD

                    def unit(lag):
                        return live or 0 <= b + kc - lag < STEPS

                    def tile_live(p):
                        return (kc - p) % 4 == 0 and (live or 0 <= b + kc - p < STEPS)

                    if ffn_live(b, c):
                        if c == 0:
                            ge(pe, xl_ready, b + GROUP)
                        ge(pe, h_ready, b + c)
                        for dst_bank, w, done in ((bk_gate, gate_t, g_ready), (bk_up, up_t, u_ready)):
                            for ii in range(2):
                                dst = dst_bank[:, ii * GT:(ii + 1) * GT].rearrange("p (m t) -> p m t", m=2)
                                cols = slice((2 * c + ii) * P, (2 * c + ii + 1) * P)
                                for k in range(KT):
                                    last = three(dst, w[:, 0, k, cols], w[:, 1, k, cols],
                                                 xh[:, :, k, :], xl[:, :, k, :], k == 0, k == KT - 1)
                            last.then_inc(done, 1)
                    if unit(3):
                        if (kc - 3) % 4 == 0:
                            ge(pe, v_ready, b + kc - 3 + 4)
                        ge(pe, pl_ready, b + kc - 2)
                        ge(pe, ao_ready, b + kc - 3)
                        u, par = (kc - 3) % 4, (kc - 3) % 2
                        vh, vl = vpart[((kc - 3) // 4) % 2]
                        for n in range(NR):
                            last = three(o_ps[:, n, 0:KD], pt[par][0][:, n, :], pt[par][1][:, n, :],
                                         vh[:, u, :], vl[:, u, :], True, True)
                        last.then_inc(o_ready, 1)
                    if unit(0):
                        if kc % 4 == 0:
                            ge(pe, stack_ready, b + kc + 4)
                        ge(pe, qkt_ready, b + kc)
                        tile, u = parts[(kc // 4) % 2], kc % 4
                        for n in range(NR + 1):
                            head = NR * u + n if n < NR else NH + u
                            last = pe.transpose(qk_ps[:, n, :], tile[:, head].rearrange("p w d -> p (w d)"), ident16[:])
                        last.then_inc(t_ready, 1)
                    if unit(2):
                        ge(pe, p_ready, b + kc - 1)
                        ge(pe, pl_ready, b + kc - 2)
                        for n in range(NR):
                            last = pe.transpose(bk_pt[:, n * P:(n + 1) * P], sm[kc % 2][:, n, :], ident[:])
                        last.then_inc(pt_ready, 1)
                    if unit(1):
                        ge(pe, qkt_ready, b + kc)
                        ge(pe, sm_ready, b + kc - 1)
                        for n in range(NR):
                            tile = qkt[(kc - 1) % 2]
                            last = pe.matmul(bk_s[:, n * P:(n + 1) * P], tile[:, n, :], tile[:, NR, :],
                                             start=True, stop=True)
                        last.then_inc(s_ready, 1)
                    if tile_live(7):
                        ge(pe, ao_ready, b + kc - 7 + 4)
                        ge(pe, xqt_ready, b + kc - 7 - 4)
                        for n in range(KT):
                            last = pe.transpose(bk_row[:, n * P:(n + 1) * P],
                                                ao[((kc - 7) // 4) % 2][:, n * P:(n + 1) * P], ident[:])
                        last.then_inc(aot_ready, 4)
                    if tile_live(8):
                        ge(pe, aol_ready, b + kc - 8 + 4)
                        for k in range(KT):
                            last = three(bk_row[:], aot[0][:, k, :], aot[1][:, k, :], wo_t[:, 0, k, :],
                                         wo_t[:, 1, k, :], k == 0, k == KT - 1)
                        last.then_inc(w_ready, 4)
                    if tile_live(13):
                        ge(pe, xd_ready, b + kc - 13 + 4)
                        ge(pe, x1_ready, b + kc - 5 if live else min(b + kc - 5, STEPS))
                        for n in range(KT):
                            last = pe.transpose(bk_row[:, n * P:(n + 1) * P], xn2[:, n * P:(n + 1) * P], ident[:])
                        last.then_inc(xdt_ready, 4)
                    if ffn_live(b, c - 2):
                        if c == 2:
                            ge(pe, yout_ready, b)
                        ge(pe, hlo_ready, b + c - 1)
                        j, par = (c - 2) % GROUP, c % 2
                        hi, lo = (hpart[par][:, w, :].rearrange("p (i t) -> p i t", i=2) for w in range(2))
                        for m in range(2):
                            for ii in range(2):
                                rows = slice(m * P, (m + 1) * P)
                                last = three(bk_acc[m][:], hi[:, ii, rows], lo[:, ii, rows],
                                             down_t[:, 0, 2 * j + ii, :], down_t[:, 1, 2 * j + ii, :],
                                             j == 0 and ii == 0, j == GROUP - 1 and ii == 1)
                            if j == GROUP - 1 and m == 0:
                                last.then_inc(acc_ready, GROUP)
                        last.then_inc(d_done, 1)

            drive(pe, body)

        @block.scalar
        def _(act):
            for t in range(3 * TILES + KT):
                act.wait_ge(w_t, t + 1)
                if t == 3 * TILES:
                    act.wait_ge(fwo_ready, 1)
                src = (bk_pt if t % 2 else bk_row)[:].rearrange("p (k r) -> p k r", k=4)
                dst, scale = weight_slot(t)
                nc.scalar.activation(dst(0), src, ACT.Identity, scale=scale).then_inc(w_hi, 1)

            def body(b):
                live = not isinstance(b, int)
                for c in range(GROUP):
                    kc = c + LEAD

                    def unit(lag):
                        return live or 0 <= b + kc - lag < STEPS

                    def tile_live(p):
                        return (kc - p) % 4 == 0 and (live or 0 <= b + kc - p < STEPS)

                    if c == 0 and ffn_live(b, 0):
                        ge(act, xs_in, b * 2 + 16)
                        ge(act, u_ready, b)
                        nc.scalar.activation(xh[:], xs[:], ACT.Copy).then_inc(xh_ready, GROUP)
                    if unit(0):
                        ge(act, t_ready, b + kc + 1)
                        ge(act, s_ready, b + kc - 1)
                        nc.scalar.activation(qkt[kc % 2], qk_ps, ACT.Copy).then_inc(qkt_ready, 1)
                    if unit(2):
                        ge(act, pt_ready, b + kc - 1)
                        ge(act, o_ready, b + kc - 3)
                        nc.scalar.activation(pt[kc % 2][0], bk_pt[:].rearrange("p (h t) -> p h t", t=P), ACT.Copy
                                             ).then_inc(ph_ready, 1)
                    if ffn_live(b, c):
                        ge(act, g_ready, b + c + 1)
                        ge(act, h_ready, b + c)
                        nc.scalar.activation(th, bk_gate[:], ACT.Tanh, scale=FTH).then_inc(th_ready, 1)
                    if ffn_live(b, c - 1):
                        ge(act, hd_ready, b + c)
                        ge(act, d_done, b + c - 2)
                        nc.scalar.activation(hpart[(c - 1) % 2][:, 0, :], hd, ACT.Copy).then_inc(hhi_ready, 1)
                    if unit(1):
                        ge(act, nmax_ready, b + kc)
                        for n in range(NR):
                            last = nc.scalar.activation(sm[(kc - 1) % 2][:, n, :], sm[(kc - 1) % 2][:, n, :], ACT.Exp,
                                                        bias=nmax[(kc - 1) % 2][:, n:n + 1])
                        last.then_inc(p_ready, 1)
                    if tile_live(-1):
                        par = ((kc + 1) // 4) % 2
                        ge(act, x_in[par], dma_count(b, kc + 1) * 2)
                        ge(act, o_ready, b + kc + 1 - 4)
                        nc.scalar.activation(vpart[par][0][:, :, 0:HD], ct[par].rearrange("p (g d) -> p g d", d=HD),
                                             ACT.Identity, scale=FV).then_inc(vhi_ready, 4)
                        ge(act, qr_ready, b + kc + 1 + 4)
                        ge(act, t_ready, b + kc + 1 - 4)
                        nc.scalar.activation(parts[par][:, :, 0, :], qc, ACT.Copy).then_inc(qhi_ready, 4)
                    if tile_live(7):
                        ge(act, aot_ready, b + kc - 7 + 4)
                        ge(act, w_ready, b + kc - 7)
                        nc.scalar.activation(aot[0], bk_row[:].rearrange("p (k t) -> p k t", t=P), ACT.Copy
                                             ).then_inc(aoh_ready, 4)
                    if tile_live(13):
                        ge(act, xdt_ready, b + kc - 13 + 4)
                        ge(act, xq_out[((kc - 17) // 4) % 2], dma_count(b, kc - 17))
                        nc.scalar.activation(xqt, bk_row[:], ACT.Copy).then_inc(xqt_ready, 4)

            drive(act, body)

        @block.gpsimd
        def _(pool):
            nc.gpsimd.memset(half_neg[:], -0.5).then_inc(su_pool, 1)
            pool.wait_ge(su_peak, 3)
            nc.gpsimd.partition_all_reduce(peak[:, PC:PC + 1], peak[:, PC:PC + 1], P, RMAX).then_inc(su_gmax, 1)
            for w in range(4):
                col = (PG, PU, PD, PO)[w]
                pool.wait_ge(su_peak, 4 + w)
                nc.gpsimd.partition_all_reduce(peak[:, col:col + 1], peak[:, col:col + 1], P, RMAX).then_inc(su_gmax, 1)
                if w == 3:
                    break
                pool.wait_ge(w_scale, w + 1)
                raw = raws[w % 2]
                for n in range(TILES + 1):
                    t = w * TILES + n
                    if n < TILES:
                        if t >= 2:
                            pool.wait_ge(w_d, t - 1)
                        nc.gpsimd.tensor_tensor(blocks(wy[t % 2]), blocks(raw[:, n, :]),
                                                spread(wblk[:, 1, n * NB:(n + 1) * NB], NB), ALU.mult
                                                ).then_inc(w_y, 1)
                    if n > 0:
                        pool.wait_ge(w_q, t)
                        if t >= 3:
                            pool.wait_ge(w_t, t - 2)
                        nc.gpsimd.tensor_tensor(blocks(wd[(t - 1) % 2]), blocks(wy[(t - 1) % 2]),
                                                spread(wblk[:, 2, (n - 1) * NB:n * NB], NB), ALU.mult
                                                ).then_inc(w_d, 1)

            def body(b):
                live = not isinstance(b, int)
                for c in range(GROUP):
                    kc = c + LEAD

                    def tile_live(p):
                        return (kc - p) % 4 == 0 and (live or 0 <= b + kc - p < STEPS)

                    if tile_live(-1):
                        ge(pool, arg_ready, b + kc + 1 + 4)
                        ge(pool, xn_ready, b + kc + 1)
                        nc.gpsimd.tensor_tensor(rstd, arg, half_neg[:], ALU.pow).then_inc(rstd_ready, 4)
                    if tile_live(9):
                        ge(pool, arg2_ready, b + kc - 9 + 4)
                        ge(pool, xn2_ready, b + kc - 9)
                        nc.gpsimd.tensor_tensor(rstd2[:, 0:1], arg2[:, 0:1], half_neg[:, 0:1], ALU.pow
                                                ).then_inc(rstd2_ready, 4)
                    if ffn_live(b, c - 1):
                        ge(pool, q_ready, b + c)
                        ge(pool, hhi_ready, b + c - 1)
                        ge(pool, hlo_ready, b + c - 1)
                        nc.gpsimd.tensor_tensor(hd, yq[(c - 1) % 2], sbc[(c - 1) % 2][:, 1, :], ALU.mult
                                                ).then_inc(hd_ready, 1)
                    if tile_live(-1):
                        ge(pool, xn_ready, b + kc + 1 + 4)
                        ge(pool, qlo_ready, b + kc + 1)
                        nc.gpsimd.tensor_tensor(qc, xn, rope_c[:], ALU.mult)
                        nc.gpsimd.tensor_tensor(halves(qs), rot(xn), halves(rope_s[:]), ALU.mult
                                                ).then_inc(qcs_ready, 4)
                        ge(pool, qhi_ready, b + kc + 1 + 4)
                        nc.gpsimd.tensor_tensor(parts[((kc + 1) // 4) % 2][:, 0:NH, 2, :], qc[:, 0:NH, :],
                                                parts[((kc + 1) // 4) % 2][:, 0:NH, 0, :], ALU.subtract)
                        nc.gpsimd.tensor_tensor(parts[((kc + 1) // 4) % 2][:, NH:NQK, 1, :], qc[:, NH:NQK, :],
                                                parts[((kc + 1) // 4) % 2][:, NH:NQK, 0, :], ALU.subtract
                                                ).then_inc(qlo_ready, 4)
                    if tile_live(10):
                        ge(pool, xsc_ready, b + kc - 10 + 4)
                        ge(pool, xd_ready, b + kc - 10)
                        nc.gpsimd.tensor_tensor(blocks(xy), blocks(xn2), spread(xsc[:, NB:2 * NB], NB), ALU.mult
                                                ).then_inc(xy_ready, 4)
                    if tile_live(12):
                        ge(pool, xqq_ready, b + kc - 12 + 4)
                        nc.gpsimd.tensor_tensor(blocks(xn2), blocks(xy), spread(xsc[:, 2 * NB:3 * NB], NB), ALU.mult
                                                ).then_inc(xd_ready, 4)
                    if ffn_live(b, c - 1):
                        ge(pool, hhi_ready, b + c)
                        nc.gpsimd.tensor_tensor(hpart[(c - 1) % 2][:, 1, :], hd, hpart[(c - 1) % 2][:, 0, :],
                                                ALU.subtract).then_inc(hlo_ready, 1)
                    if ffn_live(b, c):
                        ge(pool, sbc_ready, b + c + 1)
                        ge(pool, hd_ready, b + c - 1)
                        nc.gpsimd.tensor_tensor(yq[c % 2], hh32, sbc[c % 2][:, 0, :], ALU.mult).then_inc(y_ready, 1)

            drive(pool, body)

        @block.vector
        def _(v):
            chain = [0]

            def link(ins):
                chain[0] += 1
                ins.then_inc(su, 1)
                v.wait_ge(su, chain[0])

            def powers(c0, c1):
                link(v.tensor_scalar(pow2[:, c0:c1].bitcast(U32), peak[:, c0:c1].bitcast(U32), EXPONENT, None,
                                     ALU.bitwise_and))
                link(v.tensor_scalar(pow2[:, c0:c1], pow2[:, c0:c1], 2.0 ** -100, None, ALU.max))
                link(v.reciprocal(inv2[:, c0:c1], pow2[:, c0:c1]))

            def col(ap, n):
                return ap[:, n:n + 1]

            v.wait_ge(norm_in, 32)
            link(v.tensor_reduce(col(peak, PQ), norm_b[:, 0:NH, :].rearrange("p h d -> p (h d)"), AX, ALU.max,
                                 apply_absolute_value=True))
            link(v.tensor_reduce(col(peak, PK), norm_b[:, NH:NQK, :].rearrange("p h d -> p (h d)"), AX, ALU.max,
                                 apply_absolute_value=True))
            v.sem_inc(su_peak, 2)
            v.wait_ge(ctx_all_in, 16)
            link(v.tensor_reduce(col(peak, PC), raws[1][:, 0:B * CK // 512, :].rearrange("p n k -> p (n k)"), AX,
                                 ALU.max, apply_absolute_value=True))
            v.sem_inc(su_peak, 1)
            v.wait_ge(su_gmax, 1)
            powers(PQ, PC + 1)
            link(v.tensor_scalar(FQ, col(inv2, PQ), 2.0 ** 9, None, ALU.mult))
            link(v.tensor_scalar(FK, col(inv2, PK), 2.0 ** 10, None, ALU.mult))
            link(v.tensor_scalar(FV, col(inv2, PC), 2.0 ** 13, None, ALU.mult))
            link(v.tensor_scalar(FS, col(pow2, PQ), col(pow2, PK), 2.0 ** -19 * float(HD) ** -0.5, ALU.mult, ALU.mult))
            v.wait_ge(consts_in, 80)
            link(v.tensor_tensor(rope_c[:], norm_b, cos_sb[:].unsqueeze(1).broadcast_to([P, NQK, HD]), ALU.mult))
            link(v.tensor_tensor(halves(rope_s[:]), rot(norm_b),
                                 sin_sb[:].rearrange("p (o two e) -> p o two e", o=1, two=2)
                                 .broadcast_to([P, NQK, 2, HD // 2]), ALU.mult))
            for table in (rope_c, rope_s):
                link(v.tensor_scalar(table[:, 0:NH, :], table[:, 0:NH, :], FQ, None, ALU.mult))
                link(v.tensor_scalar(table[:, NH:NQK, :], table[:, NH:NQK, :], FK, None, ALU.mult))

            def split_lo(t):
                v.wait_ge(w_hi, t + 1)
                src = (bk_pt if t % 2 else bk_row)[:].rearrange("p (k r) -> p k r", k=4)
                dst, scale = weight_slot(t)
                v.scalar_tensor_tensor(dst(1), src, scale, dst(0), ALU.mult, ALU.subtract).then_inc(w_lo, 1)

            for w in range(4):
                c0 = (PG, PU, PD, PO)[w]
                v.wait_ge(raw_in[w], 16)
                if w < 3:
                    if w > 0:
                        v.wait_ge(w_d, TILES * w)
                    link(v.tensor_reduce(wblk[:, 0, :], raws[w % 2].rearrange("p n (q k) -> p (n q) k", k=BLOCK), AX,
                                         ALU.max, apply_absolute_value=True))
                    link(v.tensor_reduce(col(peak, c0), wblk[:, 0, :], AX, ALU.max))
                else:
                    link(v.tensor_reduce(col(peak, c0), raws[1][:, 0:KT, :].rearrange("p n k -> p (n k)"), AX,
                                         ALU.max, apply_absolute_value=True))
                v.sem_inc(su_peak, 1)
                v.wait_ge(su_gmax, 2 + w)
                powers(c0, c0 + 1)
                if w == 3:
                    link(v.tensor_scalar(FWO, col(inv2, PO), 2.0 ** 13, None, ALU.mult))
                    v.sem_inc(fwo_ready, 1)
                    break
                link(v.tensor_scalar(wblk[:, 0, :], wblk[:, 0, :], 1.0 / FP8_MAX, SCALE_FLOOR, ALU.mult, ALU.max))
                link(v.reciprocal(wblk[:, 1, :], wblk[:, 0, :]))
                v.tensor_scalar(wblk[:, 2, :], wblk[:, 0, :], col(inv2, c0), 2.0 ** 14, ALU.mult, ALU.mult
                                ).then_inc(w_scale, 1)
                for n in range(TILES + 2):
                    t = w * TILES + n
                    if n < TILES:
                        y = wy[t % 2]
                        v.wait_ge(w_y, t + 1)
                        ge(v, w_q, t)
                        link(v.tensor_scalar(wem.bitcast(U32), y.bitcast(U32), EXPONENT, None, ALU.bitwise_and))
                        link(v.tensor_scalar(wem, wem, MIN_NORMAL, MAGIC, ALU.max, ALU.mult))
                        link(v.tensor_tensor(y, y, wem, ALU.add))
                        v.tensor_tensor(y, y, wem, ALU.subtract).then_inc(w_q, 1)
                    if n >= 2:
                        split_lo(t - 2)
            for t in range(3 * TILES, 3 * TILES + KT):
                split_lo(t)
            link(v.tensor_scalar(FW, col(pow2, PC), col(pow2, PO), 2.0 ** -26, ALU.mult, ALU.mult))
            link(v.tensor_scalar(FTH, col(pow2, PG), 2.0 ** -26, None, ALU.mult))
            link(v.tensor_scalar(FFL, col(inv2, PG), col(inv2, PU), 2.0 * SCALE_FLOOR * 2.0 ** 50, ALU.mult, ALU.mult))
            link(v.tensor_scalar(FTMP, col(pow2, PG), col(pow2, PU), 2.0 ** -9, ALU.mult, ALU.mult))
            link(v.tensor_scalar(FO, FTMP, col(pow2, PD), None, ALU.mult))
            v.wait_ge(w_lo, 3 * TILES + KT)
            for par in range(2):
                link(v.memset(vpart[par][0][:, :, HD:KD], 1.0))
                link(v.memset(vpart[par][1][:, :, HD:KD], 0.0))
            v.sem_inc(setup_done, 1)

            def body(b):
                live = not isinstance(b, int)
                for c in range(GROUP):
                    kc = c + LEAD

                    def unit(lag):
                        return live or 0 <= b + kc - lag < STEPS

                    def tile_live(p):
                        return (kc - p) % 4 == 0 and (live or 0 <= b + kc - p < STEPS)

                    if c == 0 and ffn_live(b, 0):
                        ge(v, xh_ready, b + GROUP)
                        v.tensor_tensor(xl[:], xs[:], xh[:], ALU.subtract).then_inc(xl_ready, GROUP)
                    if c == 2 and ffn_live(b, -GROUP):
                        ge(v, x1f_in, b * 4)
                        for m in range(2):
                            ge(v, d_done if m else acc_ready, b)
                            v.scalar_tensor_tensor(yout[m], bk_acc[m][:], FO, x1f[m], ALU.mult, ALU.add
                                                   ).then_inc(yout_ready, 4)
                    if ffn_live(b, c - 1):
                        y = yq[(c - 1) % 2]
                        ge(v, y_ready, b + c)
                        ge(v, q_ready, b + c - 1)
                        v.tensor_scalar(em.bitcast(U32), y.bitcast(U32), EXPONENT, None, ALU.bitwise_and
                                        ).then_inc(heq, 1)
                        ge(v, heq, b * 3 + 3 * (c - 1) + 1)
                        v.tensor_scalar(em, em, MIN_NORMAL, MAGIC, ALU.max, ALU.mult).then_inc(heq, 1)
                        ge(v, heq, b * 3 + 3 * (c - 1) + 2)
                        v.tensor_tensor(y, y, em, ALU.add).then_inc(heq, 1)
                        ge(v, heq, b * 3 + 3 * (c - 1) + 3)
                        v.tensor_tensor(y, y, em, ALU.subtract).then_inc(q_ready, 1)
                    if unit(2):
                        ge(v, ph_ready, b + kc - 1)
                        v.tensor_tensor(pt[kc % 2][1], bk_pt[:].rearrange("p (h t) -> p h t", t=P), pt[kc % 2][0],
                                        ALU.subtract).then_inc(pl_ready, 1)
                    if unit(1):
                        par = (kc - 1) % 2
                        ge(v, s_ready, b + kc)
                        ge(v, pt_ready, b + kc - 2)
                        v.scalar_tensor_tensor(sm[par], bk_s[:].rearrange("p (h t) -> p h t", t=P), FS,
                                               mask[:].unsqueeze(1).broadcast_to([P, NR, P]), ALU.mult, ALU.add
                                               ).then_inc(sm_ready, 1)
                        ge(v, sm_ready, b + kc)
                        v.tensor_reduce(nmax[par], sm[par], AX, ALU.max, negate=True).then_inc(nmax_ready, 1)
                    if unit(3):
                        u = (kc - 3) % 4
                        ge(v, o_ready, b + kc - 2)
                        ge(v, ao_ready, b + kc - 3)
                        v.reciprocal(rsum.unsqueeze(2), o_ps[:, :, HD:KD]).then_inc(rsum_ready, 1)
                        ge(v, rsum_ready, b + kc - 2)
                        if u == 0:
                            ge(v, aot_ready, b + kc - 3 - 4)
                        v.tensor_tensor(ao[((kc - 3) // 4) % 2][:, u * P:(u + 1) * P].rearrange("p (h d) -> p h d", d=HD),
                                        o_ps[:, :, 0:HD], rsum.unsqueeze(2).broadcast_to([P, NR, HD]), ALU.mult
                                        ).then_inc(ao_ready, 1)
                    if ffn_live(b, c):
                        ge(v, th_ready, b + c + 1)
                        v.scalar_tensor_tensor(th, th, 1.0, bk_gate[:], ALU.add, ALU.mult).then_inc(ga_ready, 1)
                        ge(v, ga_ready, b + c + 1)
                        ge(v, u_ready, b + c + 1)
                        ge(v, y_ready, b + c)
                        ge(v, hst, b * 4 + 4 * c)
                        v.tensor_tensor(hh32, th, bk_up[:], ALU.mult).then_inc(h_ready, 1)
                        ge(v, h_ready, b + c + 1)
                        v.tensor_reduce(hmax, blocks(hh32), AX, ALU.max, apply_absolute_value=True,
                                        apply_transpose=True).then_inc(hst, 1)
                        ge(v, hst, b * 4 + 4 * c + 1)
                        v.tensor_scalar(hmax, hmax, 1.0 / FP8_MAX, FFL, ALU.mult, ALU.max).then_inc(hst, 1)
                        ge(v, hst, b * 4 + 4 * c + 2)
                        ge(v, sbc_ready, b + c)
                        v.reciprocal(hsc[:, 0:16], hmax).then_inc(hst, 1)
                        v.tensor_scalar(hsc[:, 16:32], hmax, 2.0 ** -56, None, ALU.mult).then_inc(hst, 1)
                        ge(v, hst, b * 4 + 4 * c + 4)
                        ge(v, hd_ready, b + c - 1)
                        v.transpose(blocks(sbc[c % 2].rearrange("p w n -> p (w n)")), spread(hsc, 32)
                                    ).then_inc(sbc_ready, 1)
                    if tile_live(-2):
                        par = ((kc + 2) // 4) % 2
                        ge(v, x_in[par], dma_count(b, kc + 2) * 2)
                        ge(v, xn_ready, b + kc + 2)
                        v.bn_stats(bst[:, 0:6], xt[par]).then_inc(st1, 1)
                        v.bn_stats(cbst[:, 0:6], ct[par]).then_inc(st1, 1)
                        ge(v, st1, b + kc + 2 + 2)
                        v.sem_inc(v_waited, 1)
                        v.bn_aggr(mv[:, 0:2], bst[:, 0:6]).then_inc(st1, 1)
                        v.bn_aggr(cmv[:, 0:2], cbst[:, 0:6]).then_inc(st1, 1)
                        ge(v, st1, b + kc + 2 + 4)
                        ge(v, rstd_ready, b + kc + 2)
                        v.tensor_scalar(arg[:, 0:1], mv[:, 1:2], 1.0 + EPS, EPS * EPS, ALU.mult, ALU.add)
                        v.tensor_scalar(cmv[:, 2:3], cmv[:, 0:1], cmv[:, 0:1], EPS, ALU.mult, ALU.add
                                        ).then_inc(arg_ready, 1)
                        ge(v, arg_ready, b + kc + 2 + 1)
                        v.tensor_tensor(arg[:, 1:2], cmv[:, 2:3], cmv[:, 1:2], ALU.add).then_inc(arg_ready, 3)
                    if tile_live(-1):
                        par = ((kc + 1) // 4) % 2
                        ge(v, rstd_ready, b + kc + 1 + 4)
                        ge(v, qcs_ready, b + kc + 1)
                        v.tensor_scalar(xn[:, 0:NH, :].rearrange("p h d -> p (h d)"), xt[par], mv[:, 0:1], rstd[:, 0:1],
                                        ALU.subtract, ALU.mult)
                        v.tensor_scalar(xn[:, NH:NQK, :].rearrange("p h d -> p (h d)"), ct[par], rstd[:, 1:2], None,
                                        ALU.mult).then_inc(xn_ready, 4)
                        ge(v, vhi_ready, b + kc + 1 + 4)
                        v.scalar_tensor_tensor(vpart[par][1][:, :, 0:HD], ct[par].rearrange("p (g d) -> p g d", d=HD), FV,
                                               vpart[par][0][:, :, 0:HD], ALU.mult, ALU.subtract).then_inc(v_ready, 4)
                        ge(v, qcs_ready, b + kc + 1 + 4)
                        v.tensor_tensor(qc, qc, qs, ALU.add).then_inc(qr_ready, 4)
                        ge(v, qlo_ready, b + kc + 1 + 4)
                        q = parts[par][:, 0:NH].rearrange("p h (a w) d -> p h a w d", w=2)
                        for a in range(2):
                            v.tensor_copy(q[:, :, a, 1, :], q[:, :, a, 0, :])
                        v.tensor_copy(parts[par][:, NH:NQK, 2:4, :], parts[par][:, NH:NQK, 0:2, :]
                                      ).then_inc(stack_ready, 4)
                    if tile_live(7):
                        ge(v, aoh_ready, b + kc - 7 + 4)
                        v.tensor_tensor(aot[1], bk_row[:].rearrange("p (k t) -> p k t", t=P), aot[0], ALU.subtract
                                        ).then_inc(aol_ready, 4)
                    if tile_live(8):
                        par = ((kc - 8) // 4) % 2
                        ge(v, w_ready, b + kc - 8 + 4)
                        ge(v, xr_in[par], dma_count(b, kc - 8))
                        ge(v, x1_out[par], dma_count(b, kc - 8) - 16)
                        v.scalar_tensor_tensor(x1[par], bk_row[:], FW, xr[par], ALU.mult, ALU.add).then_inc(x1_ready, 4)
                        ge(v, x1_ready, b + kc - 8 + 4)
                        ge(v, xn2_ready, b + kc - 8)
                        v.bn_stats(bst2[:, 0:6], x1[par]).then_inc(st2, 2)
                        ge(v, st2, b + kc - 8 + 2)
                        v.sem_inc(v_waited, 1)
                        v.bn_aggr(mv2[:, 0:2], bst2[:, 0:6]).then_inc(st2, 2)
                        ge(v, st2, b + kc - 8 + 4)
                        ge(v, rstd2_ready, b + kc - 8)
                        v.tensor_scalar(arg2[:, 0:1], mv2[:, 1:2], EPS, None, ALU.add).then_inc(arg2_ready, 4)
                    if tile_live(9):
                        par = ((kc - 9) // 4) % 2
                        ge(v, rstd2_ready, b + kc - 9 + 4)
                        ge(v, xdt_ready, b + kc - 9)
                        v.tensor_scalar(xn2, x1[par], mv2[:, 0:1], rstd2[:, 0:1], ALU.subtract, ALU.mult
                                        ).then_inc(xn2_ready, 4)
                        ge(v, xn2_ready, b + kc - 9 + 4)
                        ge(v, xd_ready, b + kc - 9)
                        v.tensor_reduce(xsc[:, 0:NB], blocks(xn2), AX, ALU.max, apply_absolute_value=True
                                        ).then_inc(xst, 2)
                        ge(v, xst, b + kc - 9 + 2)
                        v.tensor_scalar(xsc[:, 0:NB], xsc[:, 0:NB], 1.0 / FP8_MAX, SCALE_FLOOR, ALU.mult, ALU.max
                                        ).then_inc(xst, 2)
                        ge(v, xst, b + kc - 9 + 4)
                        v.reciprocal(xsc[:, NB:2 * NB], xsc[:, 0:NB])
                        v.tensor_scalar(xsc[:, 2 * NB:3 * NB], xsc[:, 0:NB], 2.0 ** 11, None, ALU.mult
                                        ).then_inc(xsc_ready, 4)
                    if tile_live(11):
                        ge(v, xy_ready, b + kc - 11 + 4)
                        ge(v, xqq_ready, b + kc - 11)
                        v.tensor_scalar(xem.bitcast(U32), xy.bitcast(U32), EXPONENT, None, ALU.bitwise_and
                                        ).then_inc(xeq, 1)
                        ge(v, xeq, b + kc - 11 + 1)
                        v.tensor_scalar(xem, xem, MIN_NORMAL, MAGIC, ALU.max, ALU.mult).then_inc(xeq, 1)
                        ge(v, xeq, b + kc - 11 + 2)
                        v.tensor_tensor(xy, xy, xem, ALU.add).then_inc(xeq, 2)
                        ge(v, xeq, b + kc - 11 + 4)
                        v.tensor_tensor(xy, xy, xem, ALU.subtract).then_inc(xqq_ready, 4)

            drive(v, body)


_INS = ['x', 'ctx_512', 'L0_xattn_q_norm_w', 'L0_xattn_k_norm_w', 'L0_xattn_w_out', 'L0_ffn_gate_w', 'L0_ffn_up_w',
        'L0_ffn_down_w']


def kernel(**inputs):
    import numpy as _np
    import concourse.bacc as _bacc
    from concourse import mybir as _mybir
    from concourse.bass_utils import run_bass_kernel_spmd as _run

    nc = _bacc.Bacc("TRN2", target_bir_lowering=False, num_devices=1)
    arrays, args = {}, []

    def give(name, a):
        arrays[f"in_{name}_dram"] = a
        args.append(nc.dram_tensor(f"in_{name}_dram", a.shape, _mybir.dt.from_np(a.dtype), kind="ExternalInput").ap())

    for name in _INS:
        give(name, _np.ascontiguousarray(inputs[name]))
    shape = inputs['x'].shape
    tokens, head = shape[1], 32
    inv_freq = (1.0 / _np.float32(10000.0) ** (_np.arange(0, head, 2, dtype=_np.float32) / _np.float32(head))
                ).astype(_np.float32)
    freqs = _np.outer(_np.arange(tokens, dtype=_np.float32), inv_freq).astype(_np.float32)
    give('rope_cos', _np.concatenate([_np.cos(freqs), _np.cos(freqs)], -1).astype(_np.float32))
    give('rope_sin', _np.concatenate([-_np.sin(freqs), _np.sin(freqs)], -1).astype(_np.float32))
    give('causal', _np.where(_np.tril(_np.ones((tokens, tokens), bool)), 0.0, -1e30).astype(_np.float32))
    give('eye32', _np.eye(128, dtype=_np.float32))
    give('eye16', _np.eye(128, dtype=_np.float16))
    out = nc.dram_tensor("out_0_dram", shape, _mybir.dt.float32, kind="ExternalOutput").ap()
    bass_xattn_ffn(nc, *args, out)
    r = _run(nc, [arrays], core_ids=[0])
    return r.results[0]["out_0_dram"]
```

```python
from contextlib import ExitStack

import concourse.bass as bass
from concourse import mybir


P = 128
ALU = mybir.AluOpType
ACT = mybir.ActivationFunctionType
AX = mybir.AxisListType.X
F32 = mybir.dt.float32
F16 = mybir.dt.float16
U32 = mybir.dt.uint32
RMAX = bass.bass_isa.ReduceOp.max

EPS = 1e-5
FP8_MAX = 448.0
SCALE_FLOOR = 1e-30
BLOCK = 32
MIN_NORMAL = 2.0 ** -6
MAGIC = 1.5 * 2.0 ** 20
EXPONENT = 0x7F800000
MASKED = -1e30

HD = 32
LEAD = 20
GROUP = 8


def bass_xattn_ffn(nc, x, ctx_in, q_norm_w, k_norm_w, w_out, gate_w, up_w, down_w,
                   rope_cos, rope_sin, causal, eye32, eye16, out):
    B, T, C = x.shape
    CK = ctx_in.shape[2]
    I = gate_w.shape[0]
    NH, NK = C // HD, CK // HD
    NR = NH // NK
    NQK = NH + NK
    KT = C // P
    IT = I // P
    NB = C // BLOCK
    GT = 2 * P
    STEPS = B * NK
    assert T == P and IT == 2 * GROUP and NK == 4 and CK == P and C == 512 and STEPS % GROUP == 0
    KD = HD + 1
    TILES = IT

    x_rows = x.rearrange("b t c -> (b t) c")
    ctx_rows = ctx_in.rearrange("b t c -> (b t) c")
    out_rows = out.rearrange("b t c -> (b t) c")
    x1_rows = nc.dram_tensor("x1_scratch", (B * T, C), F32, kind="Internal").ap()
    xq_rows = nc.dram_tensor("xq_scratch", (B * P, 2 * KT * P), F16, kind="Internal").ap()

    with ExitStack() as stack:
        def sb(name, shape, dt):
            return stack.enter_context(nc.sbuf_tensor(name, shape, dt))

        def bank(name):
            return stack.enter_context(nc.psum_tensor(name, [P, 512], F32))

        def sem(name):
            return stack.enter_context(nc.semaphore(name))

        gate_t = sb("gate_t", [P, 2, KT, I], F16)
        up_t = sb("up_t", [P, 2, KT, I], F16)
        down_t = sb("down_t", [P, 2, IT, C], F16)
        wo_t = sb("wo_t", [P, 2, KT, C], F16)
        rope_c = sb("rope_c", [P, NQK, HD], F32)
        rope_s = sb("rope_s", [P, NQK, HD], F32)
        mask = sb("mask", [P, P], F32)
        ident = sb("ident", [P, P], F32)
        ident16 = sb("ident16", [P, P], F16)
        cos_sb = sb("cos_sb", [P, HD], F32)
        sin_sb = sb("sin_sb", [P, HD], F32)
        half_neg = sb("half_neg", [P, 2], F32)
        peak = sb("peak", [P, 8], F32)
        pow2 = sb("pow2", [P, 8], F32)
        inv2 = sb("inv2", [P, 8], F32)
        fac = sb("fac", [P, 12], F32)
        PQ, PK, PC, PG, PU, PD, PO = range(7)
        FQ, FK, FS, FV, FW, FO, FTH, FFL, FWO, FTMP = (fac[:, n:n + 1] for n in range(10))

        AREA = 24832
        area = sb("area", [P, AREA], F32)
        taken = [0]

        def carve(words):
            at = taken[0]
            taken[0] += words
            assert taken[0] <= AREA, taken[0]
            return area[:, at:at + words]

        def carve16(count):
            return carve(count // 2).bitcast(F16)

        xs = carve16(2 * KT * GT).rearrange("p (m n) -> p m n", m=2)
        xhl = carve16(2 * KT * GT).rearrange("p (m w k t) -> p m w k t", m=2, w=2, k=KT)
        th = carve(512)
        hh32 = carve(512)
        yq = [carve(512) for _ in range(2)]
        em = carve(512)
        sbc = [carve(1024).rearrange("p (w n) -> p w n", w=2) for _ in range(2)]
        hd = carve(512)
        hpart = [carve16(1024).rearrange("p (w n) -> p w n", w=2) for _ in range(2)]
        x1f = [carve(C) for _ in range(2)]
        yout = [carve(C) for _ in range(2)]
        hmax = carve(16)
        hsc = carve(32)
        xt = [carve(C) for _ in range(2)]
        ct = [carve(CK) for _ in range(2)]
        xn = carve(NQK * HD).rearrange("p (h d) -> p h d", d=HD)
        qc = carve(NQK * HD).rearrange("p (h d) -> p h d", d=HD)
        qs = carve(NQK * HD).rearrange("p (h d) -> p h d", d=HD)
        parts = [carve16(NQK * 4 * HD).rearrange("p (h w d) -> p h w d", w=4, d=HD) for _ in range(2)]
        vpart = [[carve16(136)[:, 0:NK * KD].rearrange("p (g d) -> p g d", d=KD) for _ in range(2)]
                 for _ in range(2)]
        qkt = [carve16((NR + 1) * P).rearrange("p (h t) -> p h t", t=P) for _ in range(2)]
        sm = [carve(NR * P).rearrange("p (h t) -> p h t", t=P) for _ in range(2)]
        nmax = [carve(NR) for _ in range(2)]
        pt = [[carve16(NR * P).rearrange("p (h t) -> p h t", t=P) for _ in range(2)] for _ in range(2)]
        rsum = carve(NR)
        ao = [carve(C) for _ in range(2)]
        aot = [carve16(C).rearrange("p (k t) -> p k t", t=P) for _ in range(2)]
        xr = [carve(C) for _ in range(2)]
        x1 = [carve(C) for _ in range(2)]
        xn2 = carve(C)
        xy = carve(C)
        xem = carve(C)
        xsc = carve(3 * NB)
        xqt = carve16(2 * C).rearrange("p (w n) -> p w n", w=2)
        bst = carve(8)
        mv = carve(4)
        cbst = carve(8)
        cmv = carve(4)
        arg = carve(2)
        rstd = carve(2)
        bst2 = carve(8)
        mv2 = carve(4)
        arg2 = carve(2)
        rstd2 = carve(2)

        raws = [area[:, n * 8192:(n + 1) * 8192].rearrange("p (n k) -> p n k", k=512) for n in range(2)]
        wy = [area[:, 16384 + n * 512:16384 + (n + 1) * 512] for n in range(2)]
        wem = area[:, 17408:17920]
        wd = [area[:, 17920 + n * 512:17920 + (n + 1) * 512] for n in range(2)]
        wblk = area[:, 19456:19456 + 3 * 256].rearrange("p (w n) -> p w n", w=3)
        norm_b = area[:, 20480:20480 + NQK * HD].rearrange("p (h d) -> p h d", d=HD)

        bk_acc = [bank("bk_acc0"), bank("bk_acc1")]
        bk_gate = bank("bk_gate")
        bk_up = bank("bk_up")
        bk_qo = bank("bk_qo")
        bk_s = bank("bk_s")
        bk_pt = bank("bk_pt")
        bk_row = bank("bk_row")
        qk_ps = bk_qo[:, 0:(NR + 1) * P // 2].bitcast(F16).rearrange("p (h t) -> p h t", t=P)
        o_ps = bk_qo[:, 352:352 + NR * 36].rearrange("p (h d) -> p h d", d=36)

        consts_in = sem("consts_in")
        norm_in = sem("norm_in")
        ctx_all_in = sem("ctx_all_in")
        raw_in = [sem(f"raw_in{n}") for n in range(4)]
        su = sem("su")
        su_peak = sem("su_peak")
        su_gmax = sem("su_gmax")
        su_pool = sem("su_pool")
        w_scale = sem("w_scale")
        w_y = sem("w_y")
        w_q = sem("w_q")
        w_d = sem("w_d")
        w_t = sem("w_t")
        w_hi = sem("w_hi")
        w_lo = sem("w_lo")
        fwo_ready = sem("fwo_ready")
        sp_waited = sem("sp_waited")
        v_waited = sem("v_waited")
        setup_done = sem("setup_done")

        x_in = [sem("x_in0"), sem("x_in1")]
        xr_in = [sem("xr_in0"), sem("xr_in1")]
        st1 = sem("st1")
        arg_ready = sem("arg_ready")
        rstd_ready = sem("rstd_ready")
        xn_ready = sem("xn_ready")
        qc_ready = sem("qc_ready")
        qs_ready = sem("qs_ready")
        qr_ready = sem("qr_ready")
        qhi_ready = sem("qhi_ready")
        qlo_ready = sem("qlo_ready")
        stack_ready = sem("stack_ready")
        vhi_ready = sem("vhi_ready")
        v_ready = sem("v_ready")
        t_ready = sem("t_ready")
        qkt_ready = sem("qkt_ready")
        s_ready = sem("s_ready")
        sm_ready = sem("sm_ready")
        nmax_ready = sem("nmax_ready")
        p_ready = sem("p_ready")
        pt_ready = sem("pt_ready")
        ph_ready = sem("ph_ready")
        pl_ready = sem("pl_ready")
        o_ready = sem("o_ready")
        rsum_ready = sem("rsum_ready")
        ao_ready = sem("ao_ready")
        aot_ready = sem("aot_ready")
        aoh_ready = sem("aoh_ready")
        aol_ready = sem("aol_ready")
        w_ready = sem("w_ready")
        x1_ready = sem("x1_ready")
        st2 = sem("st2")
        arg2_ready = sem("arg2_ready")
        rstd2_ready = sem("rstd2_ready")
        xn2_ready = sem("xn2_ready")
        xst = sem("xst")
        xsc_ready = sem("xsc_ready")
        xy_ready = sem("xy_ready")
        xeq = sem("xeq")
        xqq_ready = sem("xqq_ready")
        xd_ready = sem("xd_ready")
        xdt_ready = sem("xdt_ready")
        xqh_ready = sem("xqh_ready")
        xql_ready = sem("xql_ready")
        x1_out = [sem("x1_out0"), sem("x1_out1")]
        xq_out = [sem("xq_out0"), sem("xq_out1")]

        xs_in = sem("xs_in")
        x1f_in = sem("x1f_in")
        xcopy_ready = sem("xcopy_ready")
        g_ready = sem("g_ready")
        u_ready = sem("u_ready")
        th_ready = sem("th_ready")
        ga_ready = sem("ga_ready")
        h_ready = sem("h_ready")
        hst = sem("hst")
        sbc_ready = sem("sbc_ready")
        y_ready = sem("y_ready")
        heq = sem("heq")
        z_ready = sem("z_ready")
        q_ready = sem("q_ready")
        hd_ready = sem("hd_ready")
        hhi_ready = sem("hhi_ready")
        hlo_ready = sem("hlo_ready")
        d_done = sem("d_done")
        acc_ready = sem("acc_ready")
        yout_ready = sem("yout_ready")
        y_out = [sem("y_out0"), sem("y_out1")]

        block = stack.enter_context(nc.Block())

        def ge(eng, s, value):
            if not isinstance(value, int) or value > 0:
                eng.wait_ge(s, value)

        def ffn_live(b, c):
            return not isinstance(b, int) or 0 <= b + c < STEPS

        def unit_live(b, c):
            return not isinstance(b, int) or 0 <= b + c + LEAD < STEPS

        def upto(value):
            return min(value, STEPS) if isinstance(value, int) else value

        def drive(eng, body):
            first = -4 * GROUP
            lo, hi = GROUP, STEPS - 4 * GROUP
            for b in range(first, lo, GROUP):
                body(b)
            with eng.Fori(lo // GROUP, hi // GROUP) as group:
                body(eng.snap(group * GROUP))
            for b in range(hi, STEPS + GROUP, GROUP):
                body(b)

        def dma_count(b, four_t):
            return b * 2 + 2 * four_t - 8 * ((four_t // 4) % 2) + 16

        def rot(ap):
            return ap.rearrange("p h (two e) -> p h two e", two=2)[:, :, ::-1, :]

        def halves(ap):
            return ap.rearrange("p h (two e) -> p h two e", two=2)

        def blocks(ap):
            return ap.rearrange("p (n k) -> p n k", k=BLOCK)

        def spread(ap, n):
            return ap.unsqueeze(2).broadcast_to([P, n, BLOCK])

        def weight_slot(t):
            w, n = divmod(t, TILES)
            if w < 2:
                dst = (gate_t, up_t)[w]
                return (lambda part: dst[:, part, :, n * P:(n + 1) * P]), 1.0
            if w == 2:
                rt, cc = divmod(n, 4)
                return (lambda part: down_t[:, part, 4 * cc:4 * cc + 4, rt * P:(rt + 1) * P]), 1.0
            return (lambda part: wo_t[:, part, :, n * P:(n + 1) * P]), FWO

        @block.sync
        def _(sp):
            sp.dma_start(norm_b[:, 0:NH, :].rearrange("p h d -> p (h d)"),
                         q_norm_w.rearrange("(a n) -> a n", a=1).broadcast_to([P, C])).then_inc(norm_in, 16)
            sp.dma_start(norm_b[:, NH:NQK, :].rearrange("p h d -> p (h d)"),
                         k_norm_w.rearrange("(a n) -> a n", a=1).broadcast_to([P, CK])).then_inc(norm_in, 16)
            for dst, src in ((mask, causal), (ident, eye32), (ident16, eye16), (cos_sb, rope_cos), (sin_sb, rope_sin)):
                sp.dma_start(dst[:], src).then_inc(consts_in, 16)
            sp.dma_start(raws[1][:, 0:B * CK // 512, :].rearrange("p n (b c) -> p (n b) c", c=CK),
                         ctx_in.rearrange("b t c -> t b c")).then_inc(ctx_all_in, 16)
            row_major = "(n p) k -> p n k"
            sp.dma_start(raws[0][:], gate_w.rearrange(row_major, p=P)).then_inc(raw_in[0], 16)
            sp.wait_ge(su_peak, 3)
            sp.dma_start(raws[1][:], up_w.rearrange(row_major, p=P)).then_inc(raw_in[1], 16)
            sp.wait_ge(w_y, TILES)
            sp.dma_start(raws[0].rearrange("p (n q) k -> p n (q k)", q=4),
                         down_w.rearrange(row_major, p=P)).then_inc(raw_in[2], 16)
            sp.wait_ge(w_y, 2 * TILES)
            sp.dma_start(raws[1][:, 0:KT, :], w_out.rearrange(row_major, p=P)).then_inc(raw_in[3], 16)
            sp.wait_ge(setup_done, 1)

            def tile_rows(b, k_const, p):
                return b * 32 + (k_const - p) * 32

            def body(b):
                live = not isinstance(b, int)
                for c in range(GROUP):
                    kc = c + LEAD

                    def tile_live(p):
                        return (kc - p) % 4 == 0 and (live or 0 <= b + kc - p < STEPS)

                    if tile_live(-7):
                        par = ((kc + 7) // 4) % 2
                        at = sp.snap(tile_rows(b, kc, -7)) if live else tile_rows(b, kc, -7)
                        ge(sp, xn_ready, b + kc + 7 - 4)
                        ge(sp, v_ready, b + kc + 7 - 4)
                        sp.dma_start(xt[par], x_rows[bass.ds(at, P), :]).then_inc(x_in[par], 16)
                        sp.dma_start(ct[par], ctx_rows[bass.ds(at, P), :]).then_inc(x_in[par], 16)
                    if tile_live(5):
                        par = ((kc - 5) // 4) % 2
                        at = sp.snap(tile_rows(b, kc, 5)) if live else tile_rows(b, kc, 5)
                        ge(sp, x1_ready, b + kc - 5 - 4)
                        sp.dma_start(xr[par], x_rows[bass.ds(at, P), :]).then_inc(xr_in[par], 16)
                    if tile_live(9):
                        par = ((kc - 9) // 4) % 2
                        at = sp.snap(tile_rows(b, kc, 9)) if live else tile_rows(b, kc, 9)
                        ge(sp, x1_ready, b + kc - 9 + 4)
                        sp.dma_start(x1_rows[bass.ds(at, P), :], x1[par]).then_inc(x1_out[par], 16)
                    if c == 2 and (live or 0 <= b - GROUP < STEPS):
                        for m in range(2):
                            at = sp.snap(b * 32 + (m * P - GROUP * 32)) if live else (b - GROUP) * 32 + m * P
                            ge(sp, yout_ready, b - 4 + 4 * m)
                            sp.dma_start(out_rows[bass.ds(at, P), :], yout[m]).then_inc(y_out[m], 16)
                    if c == 3 and (live or 0 <= b < STEPS):
                        for m in range(2):
                            at = sp.snap(b * 32 + m * P) if live else b * 32 + m * P
                            ge(sp, x1_out[m], b * 2 + 16)
                            ge(sp, yout_ready, b - 4 + 4 * m)
                            sp.dma_start(x1f[m], x1_rows[bass.ds(at, P), :]).then_inc(x1f_in, 16)
                    if tile_live(14):
                        par = ((kc - 14) // 4) % 2
                        at = sp.snap(tile_rows(b, kc, 14)) if live else tile_rows(b, kc, 14)
                        ge(sp, xql_ready, b + kc - 14 + 4)
                        sp.dma_start(xq_rows[bass.ds(at, P), :], xqt.rearrange("p w n -> p (w n)")
                                     ).then_inc(xq_out[par], 16)
                    if c == 6 and (live or 0 <= b + GROUP < STEPS):
                        at = sp.snap(b * 32 + GROUP * 32) if live else (b + GROUP) * 32
                        for par in range(2):
                            ge(sp, xq_out[par], b * 2 + 32)
                        sp.sem_inc(sp_waited, 1)
                        ge(sp, xcopy_ready, b + GROUP)
                        sp.dma_start(xs, xq_rows[bass.ds(at, GT), :].rearrange("(m p) n -> p m n", m=2)
                                     ).then_inc(xs_in, 16)

            drive(sp, body)
            for m in range(2):
                sp.wait_ge(y_out[m], 16 * STEPS // GROUP)
                sp.wait_ge(x1_out[m], 16 * STEPS // GROUP)
                sp.wait_ge(xq_out[m], 16 * STEPS // GROUP)

        @block.tensor
        def _(pe):
            pe.wait_ge(consts_in, 80)
            for t in range(3 * TILES + KT):
                if t < 3 * TILES:
                    pe.wait_ge(w_d, t + 1)
                    src = wd[t % 2]
                else:
                    pe.wait_ge(su_gmax, 5)
                    src = raws[1][:, t - 3 * TILES, :]
                if t >= 2:
                    pe.wait_ge(w_lo, t - 1)
                for n in range(4):
                    last = pe.transpose((bk_pt if t % 2 else bk_row)[:, n * P:(n + 1) * P],
                                        src[:, n * P:(n + 1) * P], ident[:])
                last.then_inc(w_t, 1)

            def three(dst, lhs_hi, lhs_lo, rhs_hi, rhs_lo, start, stop):
                pe.matmul(dst, lhs_hi, rhs_hi, start=start, stop=False)
                pe.matmul(dst, lhs_hi, rhs_lo, start=False, stop=False)
                return pe.matmul(dst, lhs_lo, rhs_hi, start=False, stop=stop)

            def body(b):
                live = not isinstance(b, int)
                for c in range(GROUP):
                    kc = c + LEAD

                    def unit(lag):
                        return live or 0 <= b + kc - lag < STEPS

                    def tile_live(p):
                        return (kc - p) % 4 == 0 and (live or 0 <= b + kc - p < STEPS)

                    if ffn_live(b, c):
                        if c == 0:
                            ge(pe, xcopy_ready, b + GROUP)
                        ge(pe, h_ready, b + c)
                        for dst_bank, w, done in ((bk_gate, gate_t, g_ready), (bk_up, up_t, u_ready)):
                            for ii in range(2):
                                dst = dst_bank[:, ii * GT:(ii + 1) * GT].rearrange("p (m t) -> p m t", m=2)
                                cols = slice((2 * c + ii) * P, (2 * c + ii + 1) * P)
                                for k in range(KT):
                                    last = three(dst, w[:, 0, k, cols], w[:, 1, k, cols],
                                                 xhl[:, :, 0, k, :], xhl[:, :, 1, k, :], k == 0, k == KT - 1)
                            last.then_inc(done, 1)
                    if unit(3):
                        if (kc - 3) % 4 == 0:
                            ge(pe, v_ready, b + kc - 3 + 4)
                        ge(pe, pl_ready, b + kc - 2)
                        ge(pe, ao_ready, b + kc - 3)
                        ge(pe, qkt_ready, upto(b + kc))
                        u, par = (kc - 3) % 4, (kc - 3) % 2
                        vh, vl = vpart[((kc - 3) // 4) % 2]
                        for n in range(NR):
                            last = three(o_ps[:, n, 0:KD], pt[par][0][:, n, :], pt[par][1][:, n, :],
                                         vh[:, u, :], vl[:, u, :], True, True)
                        last.then_inc(o_ready, 1)
                    if unit(0):
                        if kc % 4 == 0:
                            ge(pe, stack_ready, b + kc + 4)
                        ge(pe, qkt_ready, b + kc)
                        tile, u = parts[(kc // 4) % 2], kc % 4
                        for n in range(NR + 1):
                            head = NR * u + n if n < NR else NH + u
                            last = pe.transpose(qk_ps[:, n, :], tile[:, head].rearrange("p w d -> p (w d)"), ident16[:])
                        last.then_inc(t_ready, 1)
                    if unit(2):
                        ge(pe, p_ready, b + kc - 1)
                        ge(pe, pl_ready, b + kc - 2)
                        for n in range(NR):
                            last = pe.transpose(bk_pt[:, n * P:(n + 1) * P], sm[kc % 2][:, n, :], ident[:])
                        last.then_inc(pt_ready, 1)
                    if unit(1):
                        ge(pe, qkt_ready, b + kc)
                        ge(pe, sm_ready, b + kc - 1)
                        for n in range(NR):
                            tile = qkt[(kc - 1) % 2]
                            last = pe.matmul(bk_s[:, n * P:(n + 1) * P], tile[:, n, :], tile[:, NR, :],
                                             start=True, stop=True)
                        last.then_inc(s_ready, 1)
                    if tile_live(7):
                        ge(pe, ao_ready, b + kc - 7 + 4)
                        ge(pe, xql_ready, b + kc - 7 - 4)
                        for n in range(KT):
                            last = pe.transpose(bk_row[:, n * P:(n + 1) * P],
                                                ao[((kc - 7) // 4) % 2][:, n * P:(n + 1) * P], ident[:])
                        last.then_inc(aot_ready, 4)
                    if tile_live(8):
                        ge(pe, aol_ready, b + kc - 8 + 4)
                        for k in range(KT):
                            last = three(bk_row[:], aot[0][:, k, :], aot[1][:, k, :], wo_t[:, 0, k, :],
                                         wo_t[:, 1, k, :], k == 0, k == KT - 1)
                        last.then_inc(w_ready, 4)
                    if tile_live(13):
                        ge(pe, xd_ready, b + kc - 13 + 4)
                        ge(pe, x1_ready, upto(b + kc - 5))
                        for n in range(KT):
                            last = pe.transpose(bk_row[:, n * P:(n + 1) * P], xn2[:, n * P:(n + 1) * P], ident[:])
                        last.then_inc(xdt_ready, 4)
                    if ffn_live(b, c - 2):
                        if c == 2:
                            ge(pe, yout_ready, b)
                        ge(pe, hlo_ready, b + c - 1)
                        j, par = (c - 2) % GROUP, c % 2
                        hi, lo = (hpart[par][:, w, :].rearrange("p (i t) -> p i t", i=2) for w in range(2))
                        for m in range(2):
                            for ii in range(2):
                                rows = slice(m * P, (m + 1) * P)
                                last = three(bk_acc[m][:], hi[:, ii, rows], lo[:, ii, rows],
                                             down_t[:, 0, 2 * j + ii, :], down_t[:, 1, 2 * j + ii, :],
                                             j == 0 and ii == 0, j == GROUP - 1 and ii == 1)
                            if j == GROUP - 1 and m == 0:
                                last.then_inc(acc_ready, GROUP)
                        last.then_inc(d_done, 1)

            drive(pe, body)

        @block.scalar
        def _(act):
            for t in range(3 * TILES + KT):
                act.wait_ge(w_t, t + 1)
                if t == 3 * TILES:
                    act.wait_ge(fwo_ready, 1)
                src = (bk_pt if t % 2 else bk_row)[:].rearrange("p (k r) -> p k r", k=4)
                dst, scale = weight_slot(t)
                nc.scalar.activation(dst(0), src, ACT.Identity, scale=scale).then_inc(w_hi, 1)

            def body(b):
                live = not isinstance(b, int)
                for c in range(GROUP):
                    kc = c + LEAD

                    def unit(lag):
                        return live or 0 <= b + kc - lag < STEPS

                    def tile_live(p):
                        return (kc - p) % 4 == 0 and (live or 0 <= b + kc - p < STEPS)

                    if unit(1):
                        ge(act, t_ready, b + kc)
                        ge(act, ao_ready, b + kc - 4)
                        ge(act, s_ready, b + kc - 2)
                        nc.scalar.activation(qkt[(kc - 1) % 2], qk_ps, ACT.Copy).then_inc(qkt_ready, 1)
                    if unit(3):
                        ge(act, pt_ready, b + kc - 2)
                        ge(act, o_ready, b + kc - 4)
                        nc.scalar.activation(pt[(kc - 3) % 2][0], bk_pt[:].rearrange("p (h t) -> p h t", t=P), ACT.Copy
                                             ).then_inc(ph_ready, 1)
                    if tile_live(8):
                        ge(act, aot_ready, b + kc - 8 + 4)
                        ge(act, w_ready, b + kc - 8)
                        nc.scalar.activation(aot[0], bk_row[:].rearrange("p (k t) -> p k t", t=P), ACT.Copy
                                             ).then_inc(aoh_ready, 4)
                    if tile_live(14):
                        ge(act, xdt_ready, b + kc - 14 + 4)
                        ge(act, xq_out[((kc - 18) // 4) % 2], dma_count(b, kc - 18))
                        nc.scalar.activation(xqt[:, 0, :], bk_row[:], ACT.Copy).then_inc(xqh_ready, 4)
                    if tile_live(-1):
                        par = ((kc + 1) // 4) % 2
                        ge(act, qr_ready, b + kc + 1 + 4)
                        ge(act, t_ready, b + kc + 1 - 4)
                        nc.scalar.activation(parts[par][:, :, 0, :], qc, ACT.Copy).then_inc(qhi_ready, 4)
                    if unit(2):
                        ge(act, nmax_ready, b + kc - 1)
                        for n in range(NR):
                            last = nc.scalar.activation(sm[kc % 2][:, n, :], sm[kc % 2][:, n, :], ACT.Exp,
                                                        bias=nmax[kc % 2][:, n:n + 1])
                        last.then_inc(p_ready, 1)
                    if ffn_live(b, c):
                        ge(act, g_ready, b + c + 1)
                        ge(act, h_ready, b + c)
                        nc.scalar.activation(th, bk_gate[:], ACT.Tanh, scale=FTH).then_inc(th_ready, 1)
                    if tile_live(-1):
                        ge(act, x_in[par], dma_count(b, kc + 1) * 2)
                        ge(act, o_ready, b + kc + 1 - 4)
                        nc.scalar.activation(vpart[par][0][:, :, 0:HD], ct[par].rearrange("p (g d) -> p g d", d=HD),
                                             ACT.Identity, scale=FV).then_inc(vhi_ready, 4)
                    if ffn_live(b, c - 1):
                        ge(act, hd_ready, b + c)
                        ge(act, d_done, b + c - 2)
                        nc.scalar.activation(hpart[(c - 1) % 2][:, 0, :], hd, ACT.Copy).then_inc(hhi_ready, 1)

            drive(act, body)

        @block.gpsimd
        def _(pool):
            nc.gpsimd.memset(half_neg[:], -0.5).then_inc(su_pool, 1)
            pool.wait_ge(su_peak, 3)
            nc.gpsimd.partition_all_reduce(peak[:, PC:PC + 1], peak[:, PC:PC + 1], P, RMAX).then_inc(su_gmax, 1)
            for w in range(4):
                col = (PG, PU, PD, PO)[w]
                pool.wait_ge(su_peak, 4 + w)
                nc.gpsimd.partition_all_reduce(peak[:, col:col + 1], peak[:, col:col + 1], P, RMAX).then_inc(su_gmax, 1)
                if w == 3:
                    break
                pool.wait_ge(w_scale, w + 1)
                raw = raws[w % 2]
                for n in range(TILES + 1):
                    t = w * TILES + n
                    if n < TILES:
                        if t >= 2:
                            pool.wait_ge(w_d, t - 1)
                        nc.gpsimd.tensor_tensor(blocks(wy[t % 2]), blocks(raw[:, n, :]),
                                                spread(wblk[:, 1, n * NB:(n + 1) * NB], NB), ALU.mult
                                                ).then_inc(w_y, 1)
                    if n > 0:
                        pool.wait_ge(w_q, t)
                        if t >= 3:
                            pool.wait_ge(w_t, t - 2)
                        nc.gpsimd.tensor_tensor(blocks(wd[(t - 1) % 2]), blocks(wy[(t - 1) % 2]),
                                                spread(wblk[:, 2, (n - 1) * NB:n * NB], NB), ALU.mult
                                                ).then_inc(w_d, 1)

            def body(b):
                live = not isinstance(b, int)
                for c in range(GROUP):
                    kc = c + LEAD

                    def tile_live(p):
                        return (kc - p) % 4 == 0 and (live or 0 <= b + kc - p < STEPS)

                    if tile_live(-4):
                        ge(pool, arg_ready, b + kc + 4 + 4)
                        ge(pool, xn_ready, b + kc + 4)
                        nc.gpsimd.tensor_tensor(rstd, arg, half_neg[:], ALU.pow).then_inc(rstd_ready, 4)
                    if tile_live(-2):
                        ge(pool, xn_ready, b + kc + 2 + 4)
                        ge(pool, qr_ready, b + kc + 2)
                        nc.gpsimd.tensor_tensor(halves(qs), rot(xn), halves(rope_s[:]), ALU.mult).then_inc(qs_ready, 4)
                    if tile_live(11):
                        ge(pool, xsc_ready, b + kc - 11 + 4)
                        ge(pool, xd_ready, b + kc - 11)
                        nc.gpsimd.tensor_tensor(blocks(xy), blocks(xn2), spread(xsc[:, NB:2 * NB], NB), ALU.mult
                                                ).then_inc(xy_ready, 4)
                    if tile_live(13):
                        ge(pool, xqq_ready, b + kc - 13 + 4)
                        nc.gpsimd.tensor_tensor(blocks(xn2), blocks(xy), spread(xsc[:, 2 * NB:3 * NB], NB), ALU.mult
                                                ).then_inc(xd_ready, 4)
                    if ffn_live(b, c - 1):
                        y = yq[(c - 1) % 2]
                        ge(pool, z_ready, b + c)
                        nc.gpsimd.tensor_tensor(y, y, em, ALU.subtract).then_inc(q_ready, 1)
                        ge(pool, q_ready, b + c)
                        ge(pool, hhi_ready, b + c - 1)
                        ge(pool, hlo_ready, b + c - 1)
                        nc.gpsimd.tensor_tensor(hd, y, sbc[(c - 1) % 2][:, 1, :], ALU.mult).then_inc(hd_ready, 1)
                    if tile_live(-3):
                        ge(pool, xn_ready, b + kc + 3 + 4)
                        ge(pool, qlo_ready, b + kc + 3)
                        nc.gpsimd.tensor_tensor(qc, xn, rope_c[:], ALU.mult).then_inc(qc_ready, 4)
                    if tile_live(-1):
                        part = parts[((kc + 1) // 4) % 2]
                        ge(pool, qhi_ready, b + kc + 1 + 4)
                        nc.gpsimd.tensor_tensor(part[:, 0:NH, 2, :], qc[:, 0:NH, :], part[:, 0:NH, 0, :], ALU.subtract)
                    if ffn_live(b, c - 1):
                        ge(pool, hhi_ready, b + c)
                        nc.gpsimd.tensor_tensor(hpart[(c - 1) % 2][:, 1, :], hd, hpart[(c - 1) % 2][:, 0, :],
                                                ALU.subtract).then_inc(hlo_ready, 1)
                    if tile_live(-1):
                        nc.gpsimd.tensor_tensor(part[:, NH:NQK, 1, :], qc[:, NH:NQK, :], part[:, NH:NQK, 0, :],
                                                ALU.subtract).then_inc(qlo_ready, 4)
                    if tile_live(9):
                        ge(pool, arg2_ready, b + kc - 9 + 4)
                        ge(pool, xn2_ready, b + kc - 9)
                        nc.gpsimd.tensor_tensor(rstd2[:, 0:1], arg2[:, 0:1], half_neg[:, 0:1], ALU.pow
                                                ).then_inc(rstd2_ready, 4)
                    if ffn_live(b, c):
                        ge(pool, sbc_ready, b + c + 1)
                        ge(pool, hd_ready, b + c - 1)
                        nc.gpsimd.tensor_tensor(yq[c % 2], hh32, sbc[c % 2][:, 0, :], ALU.mult).then_inc(y_ready, 1)

            drive(pool, body)

        @block.vector
        def _(v):
            chain = [0]

            def link(ins):
                chain[0] += 1
                ins.then_inc(su, 1)
                v.wait_ge(su, chain[0])

            def powers(c0, c1):
                link(v.tensor_scalar(pow2[:, c0:c1].bitcast(U32), peak[:, c0:c1].bitcast(U32), EXPONENT, None,
                                     ALU.bitwise_and))
                link(v.tensor_scalar(pow2[:, c0:c1], pow2[:, c0:c1], 2.0 ** -100, None, ALU.max))
                link(v.reciprocal(inv2[:, c0:c1], pow2[:, c0:c1]))

            def col(ap, n):
                return ap[:, n:n + 1]

            v.wait_ge(norm_in, 32)
            link(v.tensor_reduce(col(peak, PQ), norm_b[:, 0:NH, :].rearrange("p h d -> p (h d)"), AX, ALU.max,
                                 apply_absolute_value=True))
            link(v.tensor_reduce(col(peak, PK), norm_b[:, NH:NQK, :].rearrange("p h d -> p (h d)"), AX, ALU.max,
                                 apply_absolute_value=True))
            v.sem_inc(su_peak, 2)
            v.wait_ge(ctx_all_in, 16)
            link(v.tensor_reduce(col(peak, PC), raws[1][:, 0:B * CK // 512, :].rearrange("p n k -> p (n k)"), AX,
                                 ALU.max, apply_absolute_value=True))
            v.sem_inc(su_peak, 1)
            v.wait_ge(su_gmax, 1)
            powers(PQ, PC + 1)
            link(v.tensor_scalar(FQ, col(inv2, PQ), 2.0 ** 9, None, ALU.mult))
            link(v.tensor_scalar(FK, col(inv2, PK), 2.0 ** 10, None, ALU.mult))
            link(v.tensor_scalar(FV, col(inv2, PC), 2.0 ** 13, None, ALU.mult))
            link(v.tensor_scalar(FS, col(pow2, PQ), col(pow2, PK), 2.0 ** -19 * float(HD) ** -0.5, ALU.mult, ALU.mult))
            v.wait_ge(consts_in, 80)
            link(v.tensor_tensor(rope_c[:], norm_b, cos_sb[:].unsqueeze(1).broadcast_to([P, NQK, HD]), ALU.mult))
            link(v.tensor_tensor(halves(rope_s[:]), rot(norm_b),
                                 sin_sb[:].rearrange("p (o two e) -> p o two e", o=1, two=2)
                                 .broadcast_to([P, NQK, 2, HD // 2]), ALU.mult))
            for table in (rope_c, rope_s):
                link(v.tensor_scalar(table[:, 0:NH, :], table[:, 0:NH, :], FQ, None, ALU.mult))
                link(v.tensor_scalar(table[:, NH:NQK, :], table[:, NH:NQK, :], FK, None, ALU.mult))

            def split_lo(t):
                v.wait_ge(w_hi, t + 1)
                src = (bk_pt if t % 2 else bk_row)[:].rearrange("p (k r) -> p k r", k=4)
                dst, scale = weight_slot(t)
                v.scalar_tensor_tensor(dst(1), src, scale, dst(0), ALU.mult, ALU.subtract).then_inc(w_lo, 1)

            for w in range(4):
                c0 = (PG, PU, PD, PO)[w]
                v.wait_ge(raw_in[w], 16)
                if w < 3:
                    if w > 0:
                        v.wait_ge(w_d, TILES * w)
                    link(v.tensor_reduce(wblk[:, 0, :], raws[w % 2].rearrange("p n (q k) -> p (n q) k", k=BLOCK), AX,
                                         ALU.max, apply_absolute_value=True))
                    link(v.tensor_reduce(col(peak, c0), wblk[:, 0, :], AX, ALU.max))
                else:
                    link(v.tensor_reduce(col(peak, c0), raws[1][:, 0:KT, :].rearrange("p n k -> p (n k)"), AX,
                                         ALU.max, apply_absolute_value=True))
                v.sem_inc(su_peak, 1)
                v.wait_ge(su_gmax, 2 + w)
                powers(c0, c0 + 1)
                if w == 3:
                    link(v.tensor_scalar(FWO, col(inv2, PO), 2.0 ** 13, None, ALU.mult))
                    v.sem_inc(fwo_ready, 1)
                    break
                link(v.tensor_scalar(wblk[:, 0, :], wblk[:, 0, :], 1.0 / FP8_MAX, SCALE_FLOOR, ALU.mult, ALU.max))
                link(v.reciprocal(wblk[:, 1, :], wblk[:, 0, :]))
                v.tensor_scalar(wblk[:, 2, :], wblk[:, 0, :], col(inv2, c0), 2.0 ** 14, ALU.mult, ALU.mult
                                ).then_inc(w_scale, 1)
                for n in range(TILES + 2):
                    t = w * TILES + n
                    if n < TILES:
                        y = wy[t % 2]
                        v.wait_ge(w_y, t + 1)
                        ge(v, w_q, t)
                        link(v.tensor_scalar(wem.bitcast(U32), y.bitcast(U32), EXPONENT, None, ALU.bitwise_and))
                        link(v.tensor_scalar(wem, wem, MIN_NORMAL, MAGIC, ALU.max, ALU.mult))
                        link(v.tensor_tensor(y, y, wem, ALU.add))
                        v.tensor_tensor(y, y, wem, ALU.subtract).then_inc(w_q, 1)
                    if n >= 2:
                        split_lo(t - 2)
            for t in range(3 * TILES, 3 * TILES + KT):
                split_lo(t)
            link(v.tensor_scalar(FW, col(pow2, PC), col(pow2, PO), 2.0 ** -26, ALU.mult, ALU.mult))
            link(v.tensor_scalar(FTH, col(pow2, PG), 2.0 ** -26, None, ALU.mult))
            link(v.tensor_scalar(FFL, col(inv2, PG), col(inv2, PU), 2.0 * SCALE_FLOOR * 2.0 ** 50, ALU.mult, ALU.mult))
            link(v.tensor_scalar(FTMP, col(pow2, PG), col(pow2, PU), 2.0 ** -9, ALU.mult, ALU.mult))
            link(v.tensor_scalar(FO, FTMP, col(pow2, PD), None, ALU.mult))
            v.wait_ge(w_lo, 3 * TILES + KT)
            for par in range(2):
                link(v.memset(vpart[par][0][:, :, HD:KD], 1.0))
                link(v.memset(vpart[par][1][:, :, HD:KD], 0.0))
            v.sem_inc(setup_done, 1)

            def body(b):
                live = not isinstance(b, int)
                for c in range(GROUP):
                    kc = c + LEAD

                    def unit(lag):
                        return live or 0 <= b + kc - lag < STEPS

                    def tile_live(p):
                        return (kc - p) % 4 == 0 and (live or 0 <= b + kc - p < STEPS)

                    if unit(2):
                        ge(v, s_ready, b + kc - 1)
                        ge(v, pt_ready, b + kc - 3)
                        v.scalar_tensor_tensor(sm[kc % 2], bk_s[:].rearrange("p (h t) -> p h t", t=P), FS,
                                               mask[:].unsqueeze(1).broadcast_to([P, NR, P]), ALU.mult, ALU.add
                                               ).then_inc(sm_ready, 1)
                    if unit(4):
                        ge(v, o_ready, b + kc - 3)
                        ge(v, ao_ready, b + kc - 4)
                        ge(v, qkt_ready, upto(b + kc))
                        v.reciprocal(rsum.unsqueeze(2), o_ps[:, :, HD:KD]).then_inc(rsum_ready, 1)
                    if tile_live(9):
                        xpar = ((kc - 9) // 4) % 2
                        ge(v, w_ready, b + kc - 9 + 4)
                        ge(v, xr_in[xpar], dma_count(b, kc - 9))
                        ge(v, x1_out[xpar], dma_count(b, kc - 9) - 16)
                        v.scalar_tensor_tensor(x1[xpar], bk_row[:], FW, xr[xpar], ALU.mult, ALU.add
                                               ).then_inc(x1_ready, 4)
                    if unit(2):
                        ge(v, sm_ready, b + kc - 1)
                        v.tensor_reduce(nmax[kc % 2], sm[kc % 2], AX, ALU.max, negate=True).then_inc(nmax_ready, 1)
                    if tile_live(9):
                        ge(v, x1_ready, b + kc - 9 + 4)
                        ge(v, xn2_ready, b + kc - 9)
                        v.bn_stats(bst2[:, 0:6], x1[xpar]).then_inc(st2, 2)
                    if unit(3):
                        ge(v, ph_ready, b + kc - 2)
                        v.tensor_tensor(pt[(kc - 3) % 2][1], bk_pt[:].rearrange("p (h t) -> p h t", t=P),
                                        pt[(kc - 3) % 2][0], ALU.subtract).then_inc(pl_ready, 1)
                    if tile_live(9):
                        ge(v, st2, b + kc - 9 + 2)
                        v.sem_inc(v_waited, 1)
                        v.bn_aggr(mv2[:, 0:2], bst2[:, 0:6]).then_inc(st2, 2)
                    if unit(4):
                        u = (kc - 4) % 4
                        ge(v, rsum_ready, b + kc - 3)
                        if u == 0:
                            ge(v, aot_ready, b + kc - 4 - 4)
                        v.tensor_tensor(ao[((kc - 4) // 4) % 2][:, u * P:(u + 1) * P].rearrange("p (h d) -> p h d", d=HD),
                                        o_ps[:, :, 0:HD], rsum.unsqueeze(2).broadcast_to([P, NR, HD]), ALU.mult
                                        ).then_inc(ao_ready, 1)
                    if tile_live(9):
                        ge(v, st2, b + kc - 9 + 4)
                        ge(v, rstd2_ready, b + kc - 9)
                        v.tensor_scalar(arg2[:, 0:1], mv2[:, 1:2], EPS, None, ALU.add).then_inc(arg2_ready, 4)
                    if tile_live(-3):
                        par = ((kc + 3) // 4) % 2
                        ge(v, rstd_ready, b + kc + 3 + 4)
                        ge(v, qs_ready, b + kc + 3)
                        v.tensor_scalar(xn[:, 0:NH, :].rearrange("p h d -> p (h d)"), xt[par], mv[:, 0:1], rstd[:, 0:1],
                                        ALU.subtract, ALU.mult)
                        v.tensor_scalar(xn[:, NH:NQK, :].rearrange("p h d -> p (h d)"), ct[par], rstd[:, 1:2], None,
                                        ALU.mult).then_inc(xn_ready, 4)
                    if tile_live(8):
                        ge(v, aoh_ready, b + kc - 8 + 4)
                        v.tensor_tensor(aot[1], bk_row[:].rearrange("p (k t) -> p k t", t=P), aot[0], ALU.subtract
                                        ).then_inc(aol_ready, 4)
                    if tile_live(10):
                        ge(v, rstd2_ready, b + kc - 10 + 4)
                        ge(v, xdt_ready, b + kc - 10)
                        v.tensor_scalar(xn2, x1[((kc - 10) // 4) % 2], mv2[:, 0:1], rstd2[:, 0:1], ALU.subtract, ALU.mult
                                        ).then_inc(xn2_ready, 4)
                    if tile_live(14):
                        ge(v, xqh_ready, b + kc - 14 + 4)
                        v.tensor_tensor(xqt[:, 1, :], bk_row[:], xqt[:, 0, :], ALU.subtract).then_inc(xql_ready, 4)
                    if c == 2 and ffn_live(b, -GROUP):
                        ge(v, x1f_in, b * 4)
                        for m in range(2):
                            ge(v, d_done if m else acc_ready, b)
                            ge(v, y_out[m], b * 2 - 16)
                            v.scalar_tensor_tensor(yout[m], bk_acc[m][:], FO, x1f[m], ALU.mult, ALU.add
                                                   ).then_inc(yout_ready, 4)
                    if tile_live(10):
                        ge(v, xn2_ready, b + kc - 10 + 4)
                        ge(v, xd_ready, b + kc - 10)
                        v.tensor_reduce(xsc[:, 0:NB], blocks(xn2), AX, ALU.max, apply_absolute_value=True
                                        ).then_inc(xst, 2)
                    if ffn_live(b, c - 1):
                        y = yq[(c - 1) % 2]
                        ge(v, y_ready, b + c)
                        ge(v, q_ready, b + c - 1)
                        v.tensor_scalar(em.bitcast(U32), y.bitcast(U32), EXPONENT, None, ALU.bitwise_and
                                        ).then_inc(heq, 1)
                    if ffn_live(b, c):
                        ge(v, th_ready, b + c + 1)
                        v.scalar_tensor_tensor(th, th, 1.0, bk_gate[:], ALU.add, ALU.mult).then_inc(ga_ready, 1)
                    if tile_live(10):
                        ge(v, xst, b + kc - 10 + 2)
                        v.tensor_scalar(xsc[:, 0:NB], xsc[:, 0:NB], 1.0 / FP8_MAX, SCALE_FLOOR, ALU.mult, ALU.max
                                        ).then_inc(xst, 2)
                    if ffn_live(b, c - 1):
                        ge(v, heq, b * 2 + 2 * (c - 1) + 1)
                        v.tensor_scalar(em, em, MIN_NORMAL, MAGIC, ALU.max, ALU.mult).then_inc(heq, 1)
                    if ffn_live(b, c):
                        ge(v, ga_ready, b + c + 1)
                        ge(v, u_ready, b + c + 1)
                        ge(v, y_ready, b + c)
                        ge(v, hst, b * 4 + 4 * c)
                        v.tensor_tensor(hh32, th, bk_up[:], ALU.mult).then_inc(h_ready, 1)
                    if ffn_live(b, c - 1):
                        ge(v, heq, b * 2 + 2 * (c - 1) + 2)
                        v.tensor_tensor(y, y, em, ALU.add).then_inc(z_ready, 1)
                    if tile_live(10):
                        ge(v, xst, b + kc - 10 + 4)
                        v.reciprocal(xsc[:, NB:2 * NB], xsc[:, 0:NB])
                        v.tensor_scalar(xsc[:, 2 * NB:3 * NB], xsc[:, 0:NB], 2.0 ** 11, None, ALU.mult
                                        ).then_inc(xsc_ready, 4)
                    if c == GROUP - 1 and ffn_live(b, GROUP):
                        ge(v, xs_in, b * 2 + 32)
                        ge(v, u_ready, b + GROUP)
                        v.tensor_copy(xhl.rearrange("p m w k t -> p m (w k t)"), xs).then_inc(xcopy_ready, GROUP)
                    if ffn_live(b, c):
                        ge(v, h_ready, b + c + 1)
                        v.tensor_reduce(hmax, blocks(hh32), AX, ALU.max, apply_absolute_value=True,
                                        apply_transpose=True).then_inc(hst, 1)
                    if tile_live(-5):
                        par = ((kc + 5) // 4) % 2
                        ge(v, x_in[par], dma_count(b, kc + 5) * 2)
                        ge(v, xn_ready, b + kc + 5)
                        v.bn_stats(bst[:, 0:6], xt[par]).then_inc(st1, 1)
                    if ffn_live(b, c):
                        ge(v, hst, b * 4 + 4 * c + 1)
                        v.tensor_scalar(hmax, hmax, 1.0 / FP8_MAX, FFL, ALU.mult, ALU.max).then_inc(hst, 1)
                    if tile_live(-5):
                        v.bn_stats(cbst[:, 0:6], ct[par]).then_inc(st1, 1)
                    if ffn_live(b, c):
                        ge(v, hst, b * 4 + 4 * c + 2)
                        ge(v, sbc_ready, b + c)
                        v.reciprocal(hsc[:, 0:16], hmax).then_inc(hst, 1)
                        v.tensor_scalar(hsc[:, 16:32], hmax, 2.0 ** -56, None, ALU.mult).then_inc(hst, 1)
                    if tile_live(-5):
                        ge(v, st1, b + kc + 5 + 2)
                        v.sem_inc(v_waited, 1)
                        v.bn_aggr(mv[:, 0:2], bst[:, 0:6]).then_inc(st1, 1)
                        v.bn_aggr(cmv[:, 0:2], cbst[:, 0:6]).then_inc(st1, 1)
                    if ffn_live(b, c):
                        ge(v, hst, b * 4 + 4 * c + 4)
                        ge(v, hd_ready, b + c - 1)
                        v.transpose(blocks(sbc[c % 2].rearrange("p w n -> p (w n)")), spread(hsc, 32)
                                    ).then_inc(sbc_ready, 1)
                    if tile_live(-5):
                        ge(v, st1, b + kc + 5 + 4)
                        ge(v, rstd_ready, b + kc + 5)
                        v.tensor_scalar(arg[:, 0:1], mv[:, 1:2], 1.0 + EPS, EPS * EPS, ALU.mult, ALU.add)
                        v.tensor_scalar(cmv[:, 2:3], cmv[:, 0:1], cmv[:, 0:1], EPS, ALU.mult, ALU.add
                                        ).then_inc(arg_ready, 1)
                        ge(v, arg_ready, b + kc + 5 + 1)
                        v.tensor_tensor(arg[:, 1:2], cmv[:, 2:3], cmv[:, 1:2], ALU.add).then_inc(arg_ready, 3)
                    if tile_live(-2):
                        ge(v, qc_ready, b + kc + 2 + 4)
                        ge(v, qs_ready, b + kc + 2 + 4)
                        v.tensor_tensor(qc, qc, qs, ALU.add).then_inc(qr_ready, 4)
                    if tile_live(-1):
                        par = ((kc + 1) // 4) % 2
                        ge(v, vhi_ready, b + kc + 1 + 4)
                        v.scalar_tensor_tensor(vpart[par][1][:, :, 0:HD], ct[par].rearrange("p (g d) -> p g d", d=HD), FV,
                                               vpart[par][0][:, :, 0:HD], ALU.mult, ALU.subtract).then_inc(v_ready, 4)
                        ge(v, qlo_ready, b + kc + 1 + 4)
                        q = parts[par][:, 0:NH].rearrange("p h (a w) d -> p h a w d", w=2)
                        for a in range(2):
                            v.tensor_copy(q[:, :, a, 1, :], q[:, :, a, 0, :])
                        v.tensor_copy(parts[par][:, NH:NQK, 2:4, :], parts[par][:, NH:NQK, 0:2, :]
                                      ).then_inc(stack_ready, 4)
                    if tile_live(12):
                        ge(v, xy_ready, b + kc - 12 + 4)
                        ge(v, xqq_ready, b + kc - 12)
                        v.tensor_scalar(xem.bitcast(U32), xy.bitcast(U32), EXPONENT, None, ALU.bitwise_and
                                        ).then_inc(xeq, 1)
                        ge(v, xeq, b + kc - 12 + 1)
                        v.tensor_scalar(xem, xem, MIN_NORMAL, MAGIC, ALU.max, ALU.mult).then_inc(xeq, 1)
                        ge(v, xeq, b + kc - 12 + 2)
                        v.tensor_tensor(xy, xy, xem, ALU.add).then_inc(xeq, 2)
                        ge(v, xeq, b + kc - 12 + 4)
                        v.tensor_tensor(xy, xy, xem, ALU.subtract).then_inc(xqq_ready, 4)

            drive(v, body)


_INS = ['x', 'ctx_512', 'L0_xattn_q_norm_w', 'L0_xattn_k_norm_w', 'L0_xattn_w_out', 'L0_ffn_gate_w', 'L0_ffn_up_w',
        'L0_ffn_down_w']


def kernel(**inputs):
    import numpy as _np
    import concourse.bacc as _bacc
    from concourse import mybir as _mybir
    from concourse.bass_utils import run_bass_kernel_spmd as _run

    nc = _bacc.Bacc("TRN2", target_bir_lowering=False, num_devices=1)
    arrays, args = {}, []

    def give(name, a):
        arrays[f"in_{name}_dram"] = a
        args.append(nc.dram_tensor(f"in_{name}_dram", a.shape, _mybir.dt.from_np(a.dtype), kind="ExternalInput").ap())

    for name in _INS:
        give(name, _np.ascontiguousarray(inputs[name]))
    shape = inputs['x'].shape
    tokens, head = shape[1], 32
    inv_freq = (1.0 / _np.float32(10000.0) ** (_np.arange(0, head, 2, dtype=_np.float32) / _np.float32(head))
                ).astype(_np.float32)
    freqs = _np.outer(_np.arange(tokens, dtype=_np.float32), inv_freq).astype(_np.float32)
    give('rope_cos', _np.concatenate([_np.cos(freqs), _np.cos(freqs)], -1).astype(_np.float32))
    give('rope_sin', _np.concatenate([-_np.sin(freqs), _np.sin(freqs)], -1).astype(_np.float32))
    give('causal', _np.where(_np.tril(_np.ones((tokens, tokens), bool)), 0.0, -1e30).astype(_np.float32))
    give('eye32', _np.eye(128, dtype=_np.float32))
    give('eye16', _np.eye(128, dtype=_np.float16))
    out = nc.dram_tensor("out_0_dram", shape, _mybir.dt.float32, kind="ExternalOutput").ap()
    bass_xattn_ffn(nc, *args, out)
    r = _run(nc, [arrays], core_ids=[0])
    return r.results[0]["out_0_dram"]
```

```python
from contextlib import ExitStack

import concourse.bass as bass
from concourse import mybir


P = 128
ALU = mybir.AluOpType
ACT = mybir.ActivationFunctionType
AX = mybir.AxisListType.X
F32 = mybir.dt.float32
F16 = mybir.dt.float16
U32 = mybir.dt.uint32
RMAX = bass.bass_isa.ReduceOp.max

EPS = 1e-5
FP8_MAX = 448.0
SCALE_FLOOR = 1e-30
BLOCK = 32
MIN_NORMAL = 2.0 ** -6
MAGIC = 1.5 * 2.0 ** 20
EXPONENT = 0x7F800000

HD = 32
LEAD = 21
EARLY = 7
POOL_EVERY = 6
GROUP = 8


def bass_xattn_ffn(nc, x, ctx_in, q_norm_w, k_norm_w, w_out, gate_w, up_w, down_w,
                   rope_cos, rope_sin, causal, eye32, eye16, out):
    B, T, C = x.shape
    CK = ctx_in.shape[2]
    I = gate_w.shape[0]
    NH, NK = C // HD, CK // HD
    NR = NH // NK
    NQK = NH + NK
    KT = C // P
    IT = I // P
    NB = C // BLOCK
    GT = 2 * P
    STEPS = B * NK
    assert T == P and IT == 2 * GROUP and NK == 4 and CK == P and C == 512 and STEPS % GROUP == 0
    KD = HD + 1
    TILES = IT
    EARLY_TILE = 3 * TILES - 2 * EARLY

    x_rows = x.rearrange("b t c -> (b t) c")
    ctx_rows = ctx_in.rearrange("b t c -> (b t) c")
    out_rows = out.rearrange("b t c -> (b t) c")
    x1_rows = nc.dram_tensor("x1_scratch", (B * T, C), F32, kind="Internal").ap()
    xq_rows = nc.dram_tensor("xq_scratch", (B * P, 2 * KT * P), F16, kind="Internal").ap()

    with ExitStack() as stack:
        def sb(name, shape, dt):
            return stack.enter_context(nc.sbuf_tensor(name, shape, dt))

        def bank(name):
            return stack.enter_context(nc.psum_tensor(name, [P, 512], F32))

        def sem(name):
            return stack.enter_context(nc.semaphore(name))

        gate_t = sb("gate_t", [P, 2, KT, I], F16)
        up_t = sb("up_t", [P, 2, KT, I], F16)
        down_t = sb("down_t", [P, 2, IT, C], F16)
        wo_t = sb("wo_t", [P, 2, KT, C], F16)
        rope_c = sb("rope_c", [P, NQK, HD], F32)
        rope_s = sb("rope_s", [P, NQK, HD], F32)
        mask = sb("mask", [P, P], F32)
        ident = sb("ident", [P, P], F32)
        ident16 = sb("ident16", [P, P], F16)
        cos_sb = sb("cos_sb", [P, HD], F32)
        sin_sb = sb("sin_sb", [P, HD], F32)
        half_neg = sb("half_neg", [P, 2], F32)
        floor_b = sb("floor_b", [P, 2], F32)
        peak = sb("peak", [P, 8], F32)
        pow2 = sb("pow2", [P, 8], F32)
        inv2 = sb("inv2", [P, 8], F32)
        fac = sb("fac", [P, 12], F32)
        PQ, PK, PC, PG, PU, PD, PO = range(7)
        FQ, FK, FS, FV, FW, FO, FTH, FFL, FWO, FTMP = (fac[:, n:n + 1] for n in range(10))

        AREA = 24832
        area = sb("area", [P, AREA], F32)
        PREP_AT, PREP = 8192 + 2048, 6064
        taken = {"rest": 0, "prep": PREP_AT}

        def carve(words, part="rest"):
            at = taken[part]
            if part == "rest" and at < PREP_AT + PREP and at + words > PREP_AT:
                at = PREP_AT + PREP
            taken[part] = at + words
            assert taken["rest"] <= AREA and taken["prep"] <= PREP_AT + PREP, taken
            return area[:, at:at + words]

        def carve16(count, part="rest"):
            return carve(count // 2, part).bitcast(F16)

        xs = carve16(2 * KT * GT).rearrange("p (m n) -> p m n", m=2)
        xhl = carve16(2 * KT * GT).rearrange("p (m w k t) -> p m w k t", m=2, w=2, k=KT)
        th = carve(512)
        hh32 = carve(512)
        yq = [carve(512) for _ in range(2)]
        em = carve(512)
        sbc = [carve(1024).rearrange("p (w n) -> p w n", w=2) for _ in range(2)]
        hd = carve(512)
        hpart = [carve16(1024).rearrange("p (w n) -> p w n", w=2) for _ in range(2)]
        x1f = [carve(C) for _ in range(2)]
        yout = [carve(C) for _ in range(2)]
        hmax = carve(16)
        hsc = carve(32)
        xt = [carve(C, "prep") for _ in range(2)]
        ct = [carve(CK, "prep") for _ in range(2)]
        xn = carve(NQK * HD, "prep").rearrange("p (h d) -> p h d", d=HD)
        qc = carve(NQK * HD, "prep").rearrange("p (h d) -> p h d", d=HD)
        qs = carve(NQK * HD, "prep").rearrange("p (h d) -> p h d", d=HD)
        parts = [carve16(NQK * 4 * HD, "prep").rearrange("p (h w d) -> p h w d", w=4, d=HD) for _ in range(2)]
        vpart = [[carve16(136, "prep")[:, 0:NK * KD].rearrange("p (g d) -> p g d", d=KD) for _ in range(2)]
                 for _ in range(2)]
        qkt = [carve16((NR + 1) * P).rearrange("p (h t) -> p h t", t=P) for _ in range(2)]
        sm = [carve(NR * P).rearrange("p (h t) -> p h t", t=P) for _ in range(2)]
        nmax = [carve(NR) for _ in range(2)]
        pt = [[carve16(NR * P).rearrange("p (h t) -> p h t", t=P) for _ in range(2)] for _ in range(2)]
        rsum = carve(NR)
        ao = [carve(C) for _ in range(2)]
        aot = [carve16(C).rearrange("p (k t) -> p k t", t=P) for _ in range(2)]
        xr = [carve(C) for _ in range(2)]
        x1 = [carve(C) for _ in range(2)]
        xn2 = carve(C)
        xy = carve(C)
        xem = carve(C)
        xsc = carve(3 * NB)
        xqt = carve16(2 * C).rearrange("p (w n) -> p w n", w=2)
        bst = carve(8, "prep")
        mv = carve(4, "prep")
        cbst = carve(8, "prep")
        cmv = carve(4, "prep")
        arg = carve(2, "prep")
        rstd = carve(2, "prep")
        bst2 = carve(8)
        mv2 = carve(4)
        arg2 = carve(2)
        rstd2 = carve(2)

        raws = [area[:, n * 8192:(n + 1) * 8192].rearrange("p (n k) -> p n k", k=512) for n in range(2)]
        wy = [area[:, 16384 + n * 512:16384 + (n + 1) * 512] for n in range(4)]
        wem = [area[:, 18432 + n * 512:18432 + (n + 1) * 512] for n in range(2)] + [area[:, 22656:23168]]
        wd = [area[:, 19456 + n * 512:19456 + (n + 1) * 512] for n in range(2)]
        wblk = [area[:, 20480 + n * 768:20480 + (n + 1) * 768].rearrange("p (w n) -> p w n", w=3) for n in range(2)]
        norm_b = area[:, 22016:22016 + NQK * HD].rearrange("p (h d) -> p h d", d=HD)
        ctx_all = down_t[:].rearrange("p w i c -> p (w i c)")[:, 0:2 * B * CK].bitcast(F32)

        bk_acc = [bank("bk_acc0"), bank("bk_acc1")]
        bk_gate = bank("bk_gate")
        bk_up = bank("bk_up")
        bk_qo = bank("bk_qo")
        bk_s = bank("bk_s")
        bk_pt = bank("bk_pt")
        bk_row = bank("bk_row")
        square_banks = (bk_acc[0], bk_acc[1], bk_gate, bk_up)
        qk_ps = bk_qo[:, 0:(NR + 1) * P // 2].bitcast(F16).rearrange("p (h t) -> p h t", t=P)
        o_ps = bk_qo[:, 352:352 + NR * 36].rearrange("p (h d) -> p h d", d=36)

        consts_in = sem("consts_in")
        angles_in = sem("angles_in")
        norm_in = sem("norm_in")
        ctx_all_in = sem("ctx_all_in")
        gate_in = [sem(f"gate_in{n}") for n in range(4)]
        up_in = sem("up_in")
        down_in = sem("down_in")
        wo_in = sem("wo_in")
        su = sem("su")
        su_peak = sem("su_peak")
        su_gmax = sem("su_gmax")
        w_inv = sem("w_inv")
        w_scale = sem("w_scale")
        w_y = sem("w_y")
        w_e = sem("w_e")
        w_relu = sem("w_relu")
        w_em = sem("w_em")
        w_z = sem("w_z")
        w_q = sem("w_q")
        w_qp = sem("w_qp")
        w_d = sem("w_d")
        w_t = sem("w_t")
        w_hi = sem("w_hi")
        w_lo = sem("w_lo")
        fwo_ready = sem("fwo_ready")
        floor_ready = sem("floor_ready")
        sp_waited = sem("sp_waited")
        v_waited = sem("v_waited")
        setup_done = sem("setup_done")

        x_in = [sem("x_in0"), sem("x_in1")]
        xr_in = [sem("xr_in0"), sem("xr_in1")]
        st1 = sem("st1")
        arg_ready = sem("arg_ready")
        rstd_ready = sem("rstd_ready")
        xc_ready = sem("xc_ready")
        xn_ready = sem("xn_ready")
        qc_ready = sem("qc_ready")
        qs_ready = sem("qs_ready")
        qr_ready = sem("qr_ready")
        qhi_ready = sem("qhi_ready")
        qlo_ready = sem("qlo_ready")
        stack_ready = sem("stack_ready")
        vhi_ready = sem("vhi_ready")
        v_ready = sem("v_ready")
        t_ready = sem("t_ready")
        qkt_ready = sem("qkt_ready")
        s_ready = sem("s_ready")
        sm_ready = sem("sm_ready")
        nmax_ready = sem("nmax_ready")
        p_ready = sem("p_ready")
        pt_ready = sem("pt_ready")
        ph_ready = sem("ph_ready")
        pl_ready = sem("pl_ready")
        o_ready = sem("o_ready")
        rsum_ready = sem("rsum_ready")
        ao_ready = sem("ao_ready")
        aot_ready = sem("aot_ready")
        aoh_ready = sem("aoh_ready")
        aol_ready = sem("aol_ready")
        w_ready = sem("w_ready")
        x1_ready = sem("x1_ready")
        st2 = sem("st2")
        arg2_ready = sem("arg2_ready")
        rstd2_ready = sem("rstd2_ready")
        xc2_ready = sem("xc2_ready")
        xn2_ready = sem("xn2_ready")
        xst = sem("xst")
        xsc_ready = sem("xsc_ready")
        xy_ready = sem("xy_ready")
        xe_ready = sem("xe_ready")
        xrelu = sem("xrelu")
        xem_ready = sem("xem_ready")
        xz_ready = sem("xz_ready")
        xqq_ready = sem("xqq_ready")
        xd_ready = sem("xd_ready")
        xdt_ready = sem("xdt_ready")
        xqh_ready = sem("xqh_ready")
        xql_ready = sem("xql_ready")
        x1_out = [sem("x1_out0"), sem("x1_out1")]
        xq_out = [sem("xq_out0"), sem("xq_out1")]

        xs_in = sem("xs_in")
        x1f_in = sem("x1f_in")
        xcopy_ready = sem("xcopy_ready")
        g_ready = sem("g_ready")
        u_ready = sem("u_ready")
        th_ready = sem("th_ready")
        ga_ready = sem("ga_ready")
        h_ready = sem("h_ready")
        hst = sem("hst")
        sbc_ready = sem("sbc_ready")
        y_ready = sem("y_ready")
        e_ready = sem("e_ready")
        relu_ready = sem("relu_ready")
        em_ready = sem("em_ready")
        z_ready = sem("z_ready")
        q_ready = sem("q_ready")
        hd_ready = sem("hd_ready")
        hhi_ready = sem("hhi_ready")
        hlo_ready = sem("hlo_ready")
        d_done = sem("d_done")
        acc_ready = sem("acc_ready")
        yout_ready = sem("yout_ready")
        y_out = [sem("y_out0"), sem("y_out1")]

        block = stack.enter_context(nc.Block())

        def ge(eng, s, value):
            if not isinstance(value, int) or value > 0:
                eng.wait_ge(s, value)

        def ffn_live(b, c):
            return not isinstance(b, int) or 0 <= b + c < STEPS

        def unit_live(b, c):
            return not isinstance(b, int) or 0 <= b + c + LEAD < STEPS

        def upto(value):
            return min(value, STEPS) if isinstance(value, int) else value

        def early_steps(i, step):
            n, odd = divmod(i - EARLY_TILE, 2)
            if odd == 0 and 0 <= n < EARLY:
                s = n - EARLY - LEAD
                step(s - s % GROUP, s % GROUP)

        def drive(eng, step):
            lo, hi = GROUP, STEPS - 4 * GROUP
            for s in range(-LEAD, lo):
                step(s - s % GROUP, s % GROUP)
            with eng.Fori(lo // GROUP, hi // GROUP) as group:
                b = eng.snap(group * GROUP)
                for c in range(GROUP):
                    step(b, c)
            for s in range(hi, STEPS + 2 * GROUP):
                step(s - s % GROUP, s % GROUP)

        def dma_count(b, four_t):
            return b * 2 + 2 * four_t - 8 * ((four_t // 4) % 2) + 16

        LOOK_AT = (0, 3, TILES - 6, 2 * TILES - 6, 3 * TILES - 6)
        POOL_AT = tuple(t + 1 if t else -1 for t in LOOK_AT)
        SCALE_AT = tuple(t + 2 if t else 0 for t in LOOK_AT)

        def on_pool(t):
            return t % POOL_EVERY == POOL_EVERY - 1

        def wait_q(eng, t):
            pools = (t + 1) // POOL_EVERY
            eng.wait_ge(w_qp if on_pool(t) else w_q, pools if on_pool(t) else t + 1 - pools)

        def rot(ap):
            return ap.rearrange("p h (two e) -> p h two e", two=2)[:, :, ::-1, :]

        def halves(ap):
            return ap.rearrange("p h (two e) -> p h two e", two=2)

        def blocks(ap):
            return ap.rearrange("p (n k) -> p n k", k=BLOCK)

        def spread(ap, n):
            return ap.unsqueeze(2).broadcast_to([P, n, BLOCK])

        def weight_slot(t):
            w, n = divmod(t, TILES)
            if w < 2:
                dst = (gate_t, up_t)[w]
                return (lambda part: dst[:, part, :, n * P:(n + 1) * P]), 1.0
            if w == 2:
                rt, cc = divmod(n, 4)
                return (lambda part: down_t[:, part, 4 * cc:4 * cc + 4, rt * P:(rt + 1) * P]), 1.0
            return (lambda part: wo_t[:, part, :, n * P:(n + 1) * P]), FWO

        @block.sync
        def _(sp):
            def tile_rows(b, k_const, p):
                return b * 32 + (k_const - p) * 32

            def step(b, c):
                live = not isinstance(b, int)
                kc = c + LEAD

                def tile_live(p):
                    return (kc - p) % 4 == 0 and (live or 0 <= b + kc - p < STEPS)

                if tile_live(-7):
                    par = ((kc + 7) // 4) % 2
                    at = sp.snap(tile_rows(b, kc, -7)) if live else tile_rows(b, kc, -7)
                    ge(sp, xn_ready, b + kc + 7 - 4)
                    ge(sp, v_ready, b + kc + 7 - 4)
                    sp.dma_start(xt[par], x_rows[bass.ds(at, P), :]).then_inc(x_in[par], 16)
                    sp.dma_start(ct[par], ctx_rows[bass.ds(at, P), :]).then_inc(x_in[par], 16)
                if tile_live(5):
                    par = ((kc - 5) // 4) % 2
                    at = sp.snap(tile_rows(b, kc, 5)) if live else tile_rows(b, kc, 5)
                    ge(sp, x1_ready, b + kc - 5 - 4)
                    sp.dma_start(xr[par], x_rows[bass.ds(at, P), :]).then_inc(xr_in[par], 16)
                if tile_live(10):
                    par = ((kc - 10) // 4) % 2
                    at = sp.snap(tile_rows(b, kc, 10)) if live else tile_rows(b, kc, 10)
                    ge(sp, x1_ready, b + kc - 10 + 4)
                    sp.dma_start(x1_rows[bass.ds(at, P), :], x1[par]).then_inc(x1_out[par], 16)
                if c == 2 and (live or 0 <= b - GROUP < STEPS):
                    for m in range(2):
                        at = sp.snap(b * 32 + (m * P - GROUP * 32)) if live else (b - GROUP) * 32 + m * P
                        ge(sp, yout_ready, b - 4 + 4 * m)
                        sp.dma_start(out_rows[bass.ds(at, P), :], yout[m]).then_inc(y_out[m], 16)
                if c == 3 and (live or 0 <= b < STEPS):
                    for m in range(2):
                        at = sp.snap(b * 32 + m * P) if live else b * 32 + m * P
                        ge(sp, x1_out[m], b * 2 + 16)
                        ge(sp, yout_ready, b - 4 + 4 * m)
                        sp.dma_start(x1f[m], x1_rows[bass.ds(at, P), :]).then_inc(x1f_in, 16)
                if tile_live(15):
                    par = ((kc - 15) // 4) % 2
                    at = sp.snap(tile_rows(b, kc, 15)) if live else tile_rows(b, kc, 15)
                    ge(sp, xql_ready, b + kc - 15 + 4)
                    sp.dma_start(xq_rows[bass.ds(at, P), :], xqt.rearrange("p w n -> p (w n)")
                                 ).then_inc(xq_out[par], 16)
                if c == 6 and (live or 0 <= b + GROUP < STEPS):
                    at = sp.snap(b * 32 + GROUP * 32) if live else (b + GROUP) * 32
                    for par in range(2):
                        ge(sp, xq_out[par], b * 2 + 32)
                    sp.sem_inc(sp_waited, 1)
                    ge(sp, xcopy_ready, b + GROUP)
                    sp.dma_start(xs, xq_rows[bass.ds(at, GT), :].rearrange("(m p) n -> p m n", m=2)
                                 ).then_inc(xs_in, 16)

            row_major = "(n p) k -> p n k"
            sp.dma_start(norm_b[:, 0:NH, :].rearrange("p h d -> p (h d)"),
                         q_norm_w.rearrange("(a n) -> a n", a=1).broadcast_to([P, C])).then_inc(norm_in, 16)
            sp.dma_start(norm_b[:, NH:NQK, :].rearrange("p h d -> p (h d)"),
                         k_norm_w.rearrange("(a n) -> a n", a=1).broadcast_to([P, CK])).then_inc(norm_in, 16)
            for dst, src in ((cos_sb, rope_cos), (sin_sb, rope_sin)):
                sp.dma_start(dst[:], src).then_inc(angles_in, 16)
            for q in range(4):
                sp.dma_start(raws[0][:, 4 * q:4 * q + 4, :], gate_w.rearrange(row_major, p=P)[:, 4 * q:4 * q + 4, :]
                             ).then_inc(gate_in[q], 16)
            for dst, src in ((mask, causal), (ident, eye32), (ident16, eye16)):
                sp.dma_start(dst[:], src).then_inc(consts_in, 16)
            sp.dma_start(ctx_all.rearrange("p (b c) -> p b c", c=CK),
                         ctx_in.rearrange("b t c -> t b c")).then_inc(ctx_all_in, 16)
            sp.dma_start(raws[1][:], up_w.rearrange(row_major, p=P)).then_inc(up_in, 16)
            sp.wait_ge(w_y, TILES)
            sp.dma_start(raws[0].rearrange("p (n q) k -> p n (q k)", q=4),
                         down_w.rearrange(row_major, p=P)).then_inc(down_in, 16)
            sp.wait_ge(w_y, 2 * TILES)
            sp.dma_start(raws[1][:, 0:KT, :], w_out.rearrange(row_major, p=P)).then_inc(wo_in, 16)
            for i in range(EARLY_TILE, 3 * TILES):
                early_steps(i, step)
            sp.wait_ge(setup_done, 1)

            drive(sp, step)
            for m in range(2):
                sp.wait_ge(y_out[m], 16 * STEPS // GROUP)
                sp.wait_ge(x1_out[m], 16 * STEPS // GROUP)
                sp.wait_ge(xq_out[m], 16 * STEPS // GROUP)

        @block.tensor
        def _(pe):
            def step(b, c):
                live = not isinstance(b, int)
                kc = c + LEAD

                def unit(lag):
                    return live or 0 <= b + kc - lag < STEPS

                def tile_live(p):
                    return (kc - p) % 4 == 0 and (live or 0 <= b + kc - p < STEPS)

                if ffn_live(b, c):
                    if c == 0:
                        ge(pe, xcopy_ready, b + GROUP)
                    ge(pe, h_ready, b + c)
                    for dst_bank, w, done in ((bk_gate, gate_t, g_ready), (bk_up, up_t, u_ready)):
                        for ii in range(2):
                            dst = dst_bank[:, ii * GT:(ii + 1) * GT].rearrange("p (m t) -> p m t", m=2)
                            cols = slice((2 * c + ii) * P, (2 * c + ii + 1) * P)
                            for k in range(KT):
                                last = three(dst, w[:, 0, k, cols], w[:, 1, k, cols],
                                             xhl[:, :, 0, k, :], xhl[:, :, 1, k, :], k == 0, k == KT - 1)
                        last.then_inc(done, 1)
                if unit(4):
                    if (kc - 4) % 4 == 0:
                        ge(pe, v_ready, b + kc - 4 + 4)
                    ge(pe, pl_ready, b + kc - 3)
                    ge(pe, qkt_ready, upto(b + kc))
                    ge(pe, ao_ready, b + kc - 4)
                    u, par = (kc - 4) % 4, (kc - 4) % 2
                    vh, vl = vpart[((kc - 4) // 4) % 2]
                    for n in range(NR):
                        last = three(o_ps[:, n, 0:KD], pt[par][0][:, n, :], pt[par][1][:, n, :],
                                     vh[:, u, :], vl[:, u, :], True, True)
                    last.then_inc(o_ready, 1)
                if unit(3):
                    ge(pe, p_ready, b + kc - 2)
                    ge(pe, pl_ready, b + kc - 3)
                    for n in range(NR):
                        last = pe.transpose(bk_pt[:, n * P:(n + 1) * P], sm[(kc - 1) % 2][:, n, :], ident[:])
                    last.then_inc(pt_ready, 1)
                if unit(1):
                    ge(pe, qkt_ready, b + kc)
                    ge(pe, sm_ready, b + kc - 1)
                    for n in range(NR):
                        tile = qkt[(kc - 1) % 2]
                        last = pe.matmul(bk_s[:, n * P:(n + 1) * P], tile[:, n, :], tile[:, NR, :],
                                         start=True, stop=True)
                    last.then_inc(s_ready, 1)
                if tile_live(8):
                    ge(pe, ao_ready, b + kc - 8 + 4)
                    ge(pe, xql_ready, b + kc - 8 - 4)
                    for n in range(KT):
                        last = pe.transpose(bk_row[:, n * P:(n + 1) * P],
                                            ao[((kc - 8) // 4) % 2][:, n * P:(n + 1) * P], ident[:])
                    last.then_inc(aot_ready, 4)
                if tile_live(9):
                    ge(pe, aol_ready, b + kc - 9 + 4)
                    for k in range(KT):
                        last = three(bk_row[:], aot[0][:, k, :], aot[1][:, k, :], wo_t[:, 0, k, :],
                                     wo_t[:, 1, k, :], k == 0, k == KT - 1)
                    last.then_inc(w_ready, 4)
                if ffn_live(b, c - 2):
                    if c == 2:
                        ge(pe, yout_ready, b)
                    ge(pe, hlo_ready, b + c - 1)
                    j, par = (c - 2) % GROUP, c % 2
                    hi, lo = (hpart[par][:, w, :].rearrange("p (i t) -> p i t", i=2) for w in range(2))
                    for m in range(2):
                        for ii in range(2):
                            rows = slice(m * P, (m + 1) * P)
                            last = three(bk_acc[m][:], hi[:, ii, rows], lo[:, ii, rows],
                                         down_t[:, 0, 2 * j + ii, :], down_t[:, 1, 2 * j + ii, :],
                                         j == 0 and ii == 0, j == GROUP - 1 and ii == 1)
                        if j == GROUP - 1 and m == 0:
                            last.then_inc(acc_ready, GROUP)
                    last.then_inc(d_done, 1)
                if tile_live(14):
                    ge(pe, xd_ready, b + kc - 14 + 4)
                    ge(pe, x1_ready, upto(b + kc - 6))
                    for n in range(KT):
                        last = pe.transpose(bk_row[:, n * P:(n + 1) * P], xn2[:, n * P:(n + 1) * P], ident[:])
                    last.then_inc(xdt_ready, 4)
                if unit(0):
                    if kc % 4 == 0:
                        ge(pe, stack_ready, b + kc + 4)
                    ge(pe, qkt_ready, b + kc)
                    ge(pe, ao_ready, b + kc - 3)
                    tile, u = parts[(kc // 4) % 2], kc % 4
                    for n in range(NR + 1):
                        head = NR * u + n if n < NR else NH + u
                        last = pe.transpose(qk_ps[:, n, :], tile[:, head].rearrange("p w d -> p (w d)"), ident16[:])
                    last.then_inc(t_ready, 1)

            pe.wait_ge(consts_in, 48)
            for t in range(3 * TILES + KT):
                if t < 3 * TILES:
                    pe.wait_ge(w_d, t + 1)
                    src = wd[t % 2]
                else:
                    pe.wait_ge(su_gmax, 5)
                    src = raws[1][:, t - 3 * TILES, :]
                if t >= 4:
                    pe.wait_ge(w_lo, t - 3)
                for n in range(4):
                    last = pe.transpose(square_banks[t % 4][:, n * P:(n + 1) * P],
                                        src[:, n * P:(n + 1) * P], ident[:])
                last.then_inc(w_t, 1)

            def three(dst, lhs_hi, lhs_lo, rhs_hi, rhs_lo, start, stop):
                pe.matmul(dst, lhs_hi, rhs_hi, start=start, stop=False)
                pe.matmul(dst, lhs_hi, rhs_lo, start=False, stop=False)
                return pe.matmul(dst, lhs_lo, rhs_hi, start=False, stop=stop)

            drive(pe, step)

        @block.scalar
        def _(act):
            def step(b, c):
                live = not isinstance(b, int)
                kc = c + LEAD

                def unit(lag):
                    return live or 0 <= b + kc - lag < STEPS

                def tile_live(p):
                    return (kc - p) % 4 == 0 and (live or 0 <= b + kc - p < STEPS)

                if unit(1):
                    ge(act, t_ready, b + kc)
                    ge(act, s_ready, b + kc - 2)
                    nc.scalar.activation(qkt[(kc - 1) % 2], qk_ps, ACT.Copy).then_inc(qkt_ready, 1)
                if tile_live(9):
                    ge(act, aot_ready, b + kc - 9 + 4)
                    ge(act, w_ready, b + kc - 9)
                    nc.scalar.activation(aot[0], bk_row[:].rearrange("p (k t) -> p k t", t=P), ACT.Copy
                                         ).then_inc(aoh_ready, 4)
                if tile_live(15):
                    ge(act, xdt_ready, b + kc - 15 + 4)
                    ge(act, xq_out[((kc - 19) // 4) % 2], dma_count(b, kc - 19))
                    nc.scalar.activation(xqt[:, 0, :], bk_row[:], ACT.Copy).then_inc(xqh_ready, 4)
                if ffn_live(b, c):
                    ge(act, g_ready, b + c + 1)
                    ge(act, h_ready, b + c)
                    nc.scalar.activation(th, bk_gate[:], ACT.Tanh, scale=FTH).then_inc(th_ready, 1)
                if ffn_live(b, c - 1):
                    ge(act, e_ready, b + c)
                    nc.scalar.activation(em, em, ACT.Relu, scale=MAGIC, bias=floor_b[:, 0:1]).then_inc(relu_ready, 1)
                    ge(act, relu_ready, b + c)
                    nc.scalar.activation(em, em, ACT.Identity, bias=floor_b[:, 1:2]).then_inc(em_ready, 1)
                if tile_live(-4):
                    par = ((kc + 4) // 4) % 2
                    flat = "p h d -> p (h d)"
                    ge(act, rstd_ready, b + kc + 4 + 4)
                    ge(act, qs_ready, b + kc + 4)
                    nc.scalar.activation(xn[:, 0:NH, :].rearrange(flat), xt[par], ACT.Identity, scale=-1.0,
                                         bias=mv[:, 0:1]).then_inc(xc_ready, 4)
                    nc.scalar.activation(xn[:, NH:NQK, :].rearrange(flat), ct[par], ACT.Copy, scale=rstd[:, 1:2])
                    ge(act, xc_ready, b + kc + 4 + 4)
                    nc.scalar.activation(xn[:, 0:NH, :].rearrange(flat), xn[:, 0:NH, :].rearrange(flat), ACT.Copy,
                                         scale=rstd[:, 0:1]).then_inc(xn_ready, 4)
                if tile_live(11):
                    ge(act, rstd2_ready, b + kc - 11 + 4)
                    ge(act, xdt_ready, b + kc - 11)
                    nc.scalar.activation(xn2, x1[((kc - 11) // 4) % 2], ACT.Identity, scale=-1.0, bias=mv2[:, 0:1]
                                         ).then_inc(xc2_ready, 4)
                    ge(act, xc2_ready, b + kc - 11 + 4)
                    nc.scalar.activation(xn2, xn2, ACT.Copy, scale=rstd2[:, 0:1]).then_inc(xn2_ready, 4)
                if unit(2):
                    ge(act, nmax_ready, b + kc - 1)
                    for n in range(NR):
                        last = nc.scalar.activation(sm[kc % 2][:, n, :], sm[kc % 2][:, n, :], ACT.Exp,
                                                    bias=nmax[kc % 2][:, n:n + 1])
                    last.then_inc(p_ready, 1)
                if unit(3):
                    ge(act, pt_ready, b + kc - 2)
                    ge(act, o_ready, b + kc - 4)
                    nc.scalar.activation(pt[(kc - 1) % 2][0], bk_pt[:].rearrange("p (h t) -> p h t", t=P), ACT.Copy
                                         ).then_inc(ph_ready, 1)
                if tile_live(0):
                    par = (kc // 4) % 2
                    ge(act, x_in[par], dma_count(b, kc) * 2)
                    ge(act, o_ready, b + kc - 4)
                    nc.scalar.activation(vpart[par][0][:, :, 0:HD], ct[par].rearrange("p (g d) -> p g d", d=HD),
                                         ACT.Identity, scale=FV).then_inc(vhi_ready, 4)
                if tile_live(12):
                    ge(act, xe_ready, b + kc - 12 + 4)
                    nc.scalar.activation(xem, xem, ACT.Relu, scale=MAGIC, bias=floor_b[:, 0:1]).then_inc(xrelu, 4)
                    ge(act, xrelu, b + kc - 12 + 4)
                    nc.scalar.activation(xem, xem, ACT.Identity, bias=floor_b[:, 1:2]).then_inc(xem_ready, 4)
                if tile_live(-1):
                    par = ((kc + 1) // 4) % 2
                    ge(act, qlo_ready, b + kc + 1 + 4)
                    nc.scalar.activation(parts[par][:, 0:NH, 3, :], parts[par][:, 0:NH, 2, :], ACT.Copy)
                    nc.scalar.activation(parts[par][:, NH:NQK, 3, :], parts[par][:, NH:NQK, 1, :], ACT.Copy
                                         ).then_inc(stack_ready, 4)
                if tile_live(-2):
                    par = ((kc + 2) // 4) % 2
                    ge(act, qr_ready, b + kc + 2 + 4)
                    ge(act, t_ready, b + kc + 2 - 4)
                    nc.scalar.activation(parts[par][:, 0:NH, 0:2, :],
                                         qc[:, 0:NH, :].unsqueeze(2).broadcast_to([P, NH, 2, HD]), ACT.Copy)
                    nc.scalar.activation(parts[par][:, NH:NQK, 0::2, :],
                                         qc[:, NH:NQK, :].unsqueeze(2).broadcast_to([P, NK, 2, HD]), ACT.Copy
                                         ).then_inc(qhi_ready, 4)
                if ffn_live(b, c - 1):
                    ge(act, hd_ready, b + c)
                    ge(act, d_done, b + c - 2)
                    nc.scalar.activation(hpart[(c - 1) % 2][:, 0, :], hd, ACT.Copy).then_inc(hhi_ready, 1)

            act.wait_ge(floor_ready, 1)
            for i in range(3 * TILES + KT + 3):
                early_steps(i, step)
                if i < 3 * TILES:
                    act.wait_ge(w_e, i + 1)
                    e = wem[i % 3]
                    nc.scalar.activation(e, e, ACT.Relu, scale=MAGIC, bias=floor_b[:, 0:1]).then_inc(w_relu, 1)
                    act.wait_ge(w_relu, i + 1)
                    nc.scalar.activation(e, e, ACT.Identity, bias=floor_b[:, 1:2]).then_inc(w_em, 1)
                t = i - 3
                if t >= 0:
                    act.wait_ge(w_t, t + 1)
                    if t == 3 * TILES:
                        act.wait_ge(fwo_ready, 1)
                    src = square_banks[t % 4][:].rearrange("p (k r) -> p k r", k=4)
                    dst, scale = weight_slot(t)
                    nc.scalar.activation(dst(0), src, ACT.Identity, scale=scale).then_inc(w_hi, 1)

            drive(act, step)

        @block.gpsimd
        def _(pool):
            def step(b, c):
                live = not isinstance(b, int)
                kc = c + LEAD

                def tile_live(p):
                    return (kc - p) % 4 == 0 and (live or 0 <= b + kc - p < STEPS)

                if ffn_live(b, c - 1):
                    y = yq[(c - 1) % 2]
                    ge(pool, z_ready, b + c)
                    nc.gpsimd.tensor_tensor(y, y, em, ALU.subtract).then_inc(q_ready, 1)
                    ge(pool, q_ready, b + c)
                    ge(pool, hhi_ready, b + c - 1)
                    ge(pool, hlo_ready, b + c - 1)
                    nc.gpsimd.tensor_tensor(hd, y, sbc[(c - 1) % 2][:, 1, :], ALU.mult).then_inc(hd_ready, 1)
                if ffn_live(b, c):
                    ge(pool, sbc_ready, b + c + 1)
                    ge(pool, hd_ready, b + c - 1)
                    nc.gpsimd.tensor_tensor(yq[c % 2], hh32, sbc[c % 2][:, 0, :], ALU.mult).then_inc(y_ready, 1)
                if ffn_live(b, c - 1):
                    ge(pool, hhi_ready, b + c)
                    nc.gpsimd.tensor_tensor(hpart[(c - 1) % 2][:, 1, :], hd, hpart[(c - 1) % 2][:, 0, :],
                                            ALU.subtract).then_inc(hlo_ready, 1)
                if tile_live(-5):
                    ge(pool, arg_ready, b + kc + 5 + 4)
                    ge(pool, xn_ready, b + kc + 5)
                    nc.gpsimd.tensor_tensor(rstd, arg, half_neg[:], ALU.pow).then_inc(rstd_ready, 4)
                if tile_live(-4):
                    ge(pool, xn_ready, b + kc + 4 + 4)
                    ge(pool, qr_ready, b + kc + 4)
                    nc.gpsimd.tensor_tensor(halves(qs), rot(xn), halves(rope_s[:]), ALU.mult).then_inc(qs_ready, 4)
                if tile_live(13):
                    ge(pool, xz_ready, b + kc - 13 + 4)
                    nc.gpsimd.tensor_tensor(xy, xy, xem, ALU.subtract).then_inc(xqq_ready, 4)
                if tile_live(13):
                    ge(pool, xqq_ready, b + kc - 13 + 4)
                    nc.gpsimd.tensor_tensor(blocks(xn2), blocks(xy), spread(xsc[:, 2 * NB:3 * NB], NB), ALU.mult
                                            ).then_inc(xd_ready, 4)
                if tile_live(11):
                    ge(pool, xsc_ready, b + kc - 11 + 4)
                    ge(pool, xd_ready, b + kc - 11)
                    nc.gpsimd.tensor_tensor(blocks(xy), blocks(xn2), spread(xsc[:, NB:2 * NB], NB), ALU.mult
                                            ).then_inc(xy_ready, 4)
                if tile_live(-4):
                    ge(pool, xn_ready, b + kc + 4 + 4)
                    ge(pool, qlo_ready, b + kc + 4)
                    nc.gpsimd.tensor_tensor(qc, xn, rope_c[:], ALU.mult).then_inc(qc_ready, 4)
                if tile_live(-2):
                    part = parts[((kc + 2) // 4) % 2]
                    ge(pool, qhi_ready, b + kc + 2 + 4)
                    nc.gpsimd.tensor_tensor(part[:, 0:NH, 2, :], qc[:, 0:NH, :], part[:, 0:NH, 0, :], ALU.subtract)
                if tile_live(-2):
                    nc.gpsimd.tensor_tensor(part[:, NH:NQK, 1, :], qc[:, NH:NQK, :], part[:, NH:NQK, 0, :],
                                            ALU.subtract).then_inc(qlo_ready, 4)
                if tile_live(10):
                    ge(pool, arg2_ready, b + kc - 10 + 4)
                    ge(pool, xn2_ready, b + kc - 10)
                    nc.gpsimd.tensor_tensor(rstd2[:, 0:1], arg2[:, 0:1], half_neg[:, 0:1], ALU.pow
                                            ).then_inc(rstd2_ready, 4)

            for i in range(-1, 3 * TILES + 2):
                for n in range(5):
                    if i == POOL_AT[n]:
                        col = (PG, PC, PU, PD, PO)[n]
                        pool.wait_ge(su_peak, n + 1)
                        nc.gpsimd.partition_all_reduce(peak[:, col:col + 1], peak[:, col:col + 1], P, RMAX
                                                       ).then_inc(su_gmax, 1)
                if i + 1 < 3 * TILES:
                    w, n = divmod(i + 1, TILES)
                    if n == 0:
                        pool.wait_ge(w_inv, w + 1)
                    if i >= 3:
                        pool.wait_ge(w_d, i - 2)
                    nc.gpsimd.tensor_tensor(blocks(wy[(i + 1) % 4]), blocks(raws[w % 2][:, n, :]),
                                            spread(wblk[w % 2][:, 1, n * NB:(n + 1) * NB], NB), ALU.mult
                                            ).then_inc(w_y, 1)
                early_steps(i, step)
                t = i - 2
                if t >= 0:
                    w, n = divmod(t, TILES)
                    if n == 0:
                        pool.wait_ge(w_scale, w + 1)
                    if on_pool(t):
                        pool.wait_ge(w_z, t + 1)
                        nc.gpsimd.tensor_tensor(wy[t % 4], wy[t % 4], wem[t % 3], ALU.subtract).then_inc(w_qp, 1)
                    wait_q(pool, t)
                    if t >= 2:
                        pool.wait_ge(w_t, t - 1)
                    nc.gpsimd.tensor_tensor(blocks(wd[t % 2]), blocks(wy[t % 4]),
                                            spread(wblk[w % 2][:, 2, n * NB:(n + 1) * NB], NB), ALU.mult
                                            ).then_inc(w_d, 1)
            drive(pool, step)

        @block.vector
        def _(v):
            def step(b, c):
                live = not isinstance(b, int)
                kc = c + LEAD

                def unit(lag):
                    return live or 0 <= b + kc - lag < STEPS

                def tile_live(p):
                    return (kc - p) % 4 == 0 and (live or 0 <= b + kc - p < STEPS)

                if unit(2):
                    ge(v, s_ready, b + kc - 1)
                    ge(v, pt_ready, b + kc - 3)
                    v.scalar_tensor_tensor(sm[kc % 2], bk_s[:].rearrange("p (h t) -> p h t", t=P), FS,
                                           mask[:].unsqueeze(1).broadcast_to([P, NR, P]), ALU.mult, ALU.add
                                           ).then_inc(sm_ready, 1)
                if unit(4):
                    ge(v, ph_ready, b + kc - 3)
                    v.tensor_tensor(pt[(kc - 4) % 2][1], bk_pt[:].rearrange("p (h t) -> p h t", t=P),
                                    pt[(kc - 4) % 2][0], ALU.subtract).then_inc(pl_ready, 1)
                if unit(2):
                    ge(v, sm_ready, b + kc - 1)
                    v.tensor_reduce(nmax[kc % 2], sm[kc % 2], AX, ALU.max, negate=True).then_inc(nmax_ready, 1)
                if ffn_live(b, c - 1):
                    y = yq[(c - 1) % 2]
                    ge(v, y_ready, b + c)
                    ge(v, q_ready, b + c - 1)
                    v.tensor_scalar(em.bitcast(U32), y.bitcast(U32), EXPONENT, None, ALU.bitwise_and
                                    ).then_inc(e_ready, 1)
                if tile_live(1):
                    par = ((kc - 1) // 4) % 2
                    ge(v, vhi_ready, b + kc - 1 + 4)
                    v.scalar_tensor_tensor(vpart[par][1][:, :, 0:HD], ct[par].rearrange("p (g d) -> p g d", d=HD), FV,
                                           vpart[par][0][:, :, 0:HD], ALU.mult, ALU.subtract).then_inc(v_ready, 4)
                if tile_live(10):
                    xpar = ((kc - 10) // 4) % 2
                    ge(v, w_ready, b + kc - 10 + 4)
                    ge(v, xr_in[xpar], dma_count(b, kc - 10))
                    ge(v, x1_out[xpar], dma_count(b, kc - 10) - 16)
                    v.scalar_tensor_tensor(x1[xpar], bk_row[:], FW, xr[xpar], ALU.mult, ALU.add
                                           ).then_inc(x1_ready, 4)
                    ge(v, x1_ready, b + kc - 10 + 4)
                    ge(v, xn2_ready, b + kc - 10)
                    v.bn_stats(bst2[:, 0:6], x1[xpar]).then_inc(st2, 2)
                    ge(v, st2, b + kc - 10 + 2)
                    v.sem_inc(v_waited, 1)
                    v.bn_aggr(mv2[:, 0:2], bst2[:, 0:6]).then_inc(st2, 2)
                    ge(v, st2, b + kc - 10 + 4)
                    ge(v, rstd2_ready, b + kc - 10)
                    v.tensor_scalar(arg2[:, 0:1], mv2[:, 1:2], EPS, None, ALU.add).then_inc(arg2_ready, 4)
                if tile_live(9):
                    ge(v, aoh_ready, b + kc - 9 + 4)
                    v.tensor_tensor(aot[1], bk_row[:].rearrange("p (k t) -> p k t", t=P), aot[0], ALU.subtract
                                    ).then_inc(aol_ready, 4)
                if tile_live(13):
                    ge(v, xem_ready, b + kc - 13 + 4)
                    v.tensor_tensor(xy, xy, xem, ALU.add).then_inc(xz_ready, 4)
                if tile_live(15):
                    ge(v, xqh_ready, b + kc - 15 + 4)
                    v.tensor_tensor(xqt[:, 1, :], bk_row[:], xqt[:, 0, :], ALU.subtract).then_inc(xql_ready, 4)
                if c == 2 and ffn_live(b, -GROUP):
                    ge(v, x1f_in, b * 4)
                    for m in range(2):
                        ge(v, d_done if m else acc_ready, b)
                        ge(v, y_out[m], b * 2 - 16)
                        v.scalar_tensor_tensor(yout[m], bk_acc[m][:], FO, x1f[m], ALU.mult, ALU.add
                                               ).then_inc(yout_ready, 4)
                if ffn_live(b, c):
                    ge(v, th_ready, b + c + 1)
                    v.scalar_tensor_tensor(th, th, 1.0, bk_gate[:], ALU.add, ALU.mult).then_inc(ga_ready, 1)
                if ffn_live(b, c):
                    ge(v, ga_ready, b + c + 1)
                    ge(v, u_ready, b + c + 1)
                    ge(v, y_ready, b + c)
                    ge(v, hst, b * 4 + 4 * c)
                    v.tensor_tensor(hh32, th, bk_up[:], ALU.mult).then_inc(h_ready, 1)
                if unit(4):
                    ge(v, o_ready, b + kc - 3)
                    ge(v, ao_ready, b + kc - 4)
                    v.reciprocal(rsum.unsqueeze(2), o_ps[:, :, HD:KD]).then_inc(rsum_ready, 1)
                if unit(4):
                    u = (kc - 4) % 4
                    ge(v, rsum_ready, b + kc - 3)
                    if u == 0:
                        ge(v, aot_ready, b + kc - 4 - 4)
                    v.tensor_tensor(ao[((kc - 4) // 4) % 2][:, u * P:(u + 1) * P].rearrange("p (h d) -> p h d", d=HD),
                                    o_ps[:, :, 0:HD], rsum.unsqueeze(2).broadcast_to([P, NR, HD]), ALU.mult
                                    ).then_inc(ao_ready, 1)
                if ffn_live(b, c - 1):
                    ge(v, em_ready, b + c)
                    v.tensor_tensor(y, y, em, ALU.add).then_inc(z_ready, 1)
                if c == GROUP - 1 and ffn_live(b, GROUP):
                    ge(v, xs_in, b * 2 + 32)
                    ge(v, u_ready, b + GROUP)
                    v.tensor_copy(xhl.rearrange("p m w k t -> p m (w k t)"), xs).then_inc(xcopy_ready, GROUP)
                if ffn_live(b, c):
                    ge(v, h_ready, b + c + 1)
                    v.tensor_reduce(hmax, blocks(hh32), AX, ALU.max, apply_absolute_value=True,
                                    apply_transpose=True).then_inc(hst, 1)
                if tile_live(12):
                    ge(v, xy_ready, b + kc - 12 + 4)
                    ge(v, xqq_ready, b + kc - 12)
                    v.tensor_scalar(xem.bitcast(U32), xy.bitcast(U32), EXPONENT, None, ALU.bitwise_and
                                    ).then_inc(xe_ready, 4)
                if tile_live(-6):
                    par = ((kc + 6) // 4) % 2
                    ge(v, x_in[par], dma_count(b, kc + 6) * 2)
                    ge(v, xn_ready, b + kc + 6)
                    v.bn_stats(bst[:, 0:6], xt[par]).then_inc(st1, 1)
                    v.bn_stats(cbst[:, 0:6], ct[par]).then_inc(st1, 1)
                if ffn_live(b, c):
                    ge(v, hst, b * 4 + 4 * c + 1)
                    v.tensor_scalar(hmax, hmax, 1.0 / FP8_MAX, FFL, ALU.mult, ALU.max).then_inc(hst, 1)
                if tile_live(-6):
                    ge(v, st1, b + kc + 6 + 2)
                    v.sem_inc(v_waited, 1)
                    v.bn_aggr(mv[:, 0:2], bst[:, 0:6]).then_inc(st1, 1)
                    v.bn_aggr(cmv[:, 0:2], cbst[:, 0:6]).then_inc(st1, 1)
                if ffn_live(b, c):
                    ge(v, hst, b * 4 + 4 * c + 2)
                    ge(v, sbc_ready, b + c)
                    v.reciprocal(hsc[:, 0:16], hmax).then_inc(hst, 1)
                    v.tensor_scalar(hsc[:, 16:32], hmax, 2.0 ** -56, None, ALU.mult).then_inc(hst, 1)
                if tile_live(11):
                    ge(v, xn2_ready, b + kc - 11 + 4)
                    ge(v, xd_ready, b + kc - 11)
                    v.tensor_reduce(xsc[:, 0:NB], blocks(xn2), AX, ALU.max, apply_absolute_value=True
                                    ).then_inc(xst, 2)
                if tile_live(-3):
                    ge(v, qc_ready, b + kc + 3 + 4)
                    ge(v, qs_ready, b + kc + 3 + 4)
                    v.tensor_tensor(qc, qc, qs, ALU.add).then_inc(qr_ready, 4)
                if ffn_live(b, c):
                    ge(v, hst, b * 4 + 4 * c + 4)
                    ge(v, hd_ready, b + c - 1)
                    v.transpose(blocks(sbc[c % 2].rearrange("p w n -> p (w n)")), spread(hsc, 32)
                                ).then_inc(sbc_ready, 1)
                if tile_live(11):
                    ge(v, xst, b + kc - 11 + 2)
                    v.tensor_scalar(xsc[:, 0:NB], xsc[:, 0:NB], 1.0 / FP8_MAX, SCALE_FLOOR, ALU.mult, ALU.max
                                    ).then_inc(xst, 2)
                if tile_live(11):
                    ge(v, xst, b + kc - 11 + 4)
                    v.reciprocal(xsc[:, NB:2 * NB], xsc[:, 0:NB])
                    v.tensor_scalar(xsc[:, 2 * NB:3 * NB], xsc[:, 0:NB], -2.0 ** 11, None, ALU.mult
                                    ).then_inc(xsc_ready, 4)
                if tile_live(-6):
                    ge(v, st1, b + kc + 6 + 4)
                    ge(v, rstd_ready, b + kc + 6)
                    v.tensor_scalar(arg[:, 0:1], mv[:, 1:2], 1.0 + EPS, EPS * EPS, ALU.mult, ALU.add)
                    v.tensor_scalar(cmv[:, 2:3], cmv[:, 0:1], cmv[:, 0:1], EPS, ALU.mult, ALU.add
                                    ).then_inc(arg_ready, 1)
                    ge(v, arg_ready, b + kc + 6 + 1)
                    v.tensor_tensor(arg[:, 1:2], cmv[:, 2:3], cmv[:, 1:2], ALU.add).then_inc(arg_ready, 3)

            chain = [0]

            def link(ins):
                chain[0] += 1
                ins.then_inc(su, 1)
                v.wait_ge(su, chain[0])

            def powers(c0, c1):
                link(v.tensor_scalar(pow2[:, c0:c1].bitcast(U32), peak[:, c0:c1].bitcast(U32), EXPONENT, None,
                                     ALU.bitwise_and))
                link(v.tensor_scalar(pow2[:, c0:c1], pow2[:, c0:c1], 2.0 ** -100, None, ALU.max))
                link(v.reciprocal(inv2[:, c0:c1], pow2[:, c0:c1]))

            def col(ap, n):
                return ap[:, n:n + 1]

            v.memset(half_neg[:], -0.5)
            v.memset(floor_b[:, 0:1], -MIN_NORMAL * MAGIC)
            v.memset(floor_b[:, 1:2], MIN_NORMAL * MAGIC).then_inc(floor_ready, 1)

            def look_over(n):
                if n == 1:
                    v.wait_ge(ctx_all_in, 16)
                    link(v.tensor_reduce(col(peak, PC), ctx_all, AX, ALU.max, apply_absolute_value=True))
                    v.sem_inc(su_peak, 1)
                elif n == 4:
                    v.wait_ge(wo_in, 16)
                    link(v.tensor_reduce(col(peak, PO), raws[1][:, 0:KT, :].rearrange("p n k -> p (n k)"), AX,
                                         ALU.max, apply_absolute_value=True))
                    v.sem_inc(su_peak, 1)
                else:
                    w = max(n - 1, 0)
                    blk, raw = wblk[w % 2], raws[w % 2].rearrange("p n (q k) -> p (n q) k", k=BLOCK)
                    if w == 2:
                        v.wait_ge(w_d, TILES)
                    chunks = 4 if w == 0 else 1
                    for q in range(chunks):
                        v.wait_ge(gate_in[q] if w == 0 else (up_in, down_in)[w - 1], 16)
                        rows = slice(q * TILES * NB // chunks, (q + 1) * TILES * NB // chunks)
                        link(v.tensor_reduce(blk[:, 0, rows], raw[:, rows, :], AX, ALU.max, apply_absolute_value=True))
                    link(v.tensor_reduce(col(peak, (PG, PU, PD)[w]), blk[:, 0, :], AX, ALU.max))
                    v.sem_inc(su_peak, 1)
                    link(v.tensor_scalar(blk[:, 0, :], blk[:, 0, :], 1.0 / FP8_MAX, SCALE_FLOOR, ALU.mult, ALU.max))
                    link(v.reciprocal(blk[:, 1, :], blk[:, 0, :]))
                    v.sem_inc(w_inv, 1)

            def make_scalings(n):
                v.wait_ge(su_gmax, n + 1)
                if n == 1:
                    powers(PC, PC + 1)
                    link(v.tensor_scalar(FV, col(inv2, PC), 2.0 ** 13, None, ALU.mult))
                elif n == 4:
                    powers(PO, PO + 1)
                    link(v.tensor_scalar(FWO, col(inv2, PO), 2.0 ** 13, None, ALU.mult))
                    v.sem_inc(fwo_ready, 1)
                    link(v.tensor_scalar(FW, col(pow2, PC), col(pow2, PO), 2.0 ** -26, ALU.mult, ALU.mult))
                    link(v.tensor_scalar(FTH, col(pow2, PG), 2.0 ** -26, None, ALU.mult))
                    link(v.tensor_scalar(FFL, col(inv2, PG), col(inv2, PU), 2.0 * SCALE_FLOOR * 2.0 ** 50,
                                         ALU.mult, ALU.mult))
                    link(v.tensor_scalar(FTMP, col(pow2, PG), col(pow2, PU), 2.0 ** -9, ALU.mult, ALU.mult))
                    link(v.tensor_scalar(FO, FTMP, col(pow2, PD), None, ALU.mult))
                    v.wait_ge(consts_in, 48)
                    v.wait_ge(w_y, 2 * TILES)
                    for par in range(2):
                        link(v.memset(vpart[par][0][:, :, HD:KD], 1.0))
                        link(v.memset(vpart[par][1][:, :, HD:KD], 0.0))
                else:
                    w = max(n - 1, 0)
                    c0, blk = (PG, PU, PD)[w], wblk[w % 2]
                    powers(c0, c0 + 1)
                    link(v.tensor_scalar(blk[:, 2, :], blk[:, 0, :], col(inv2, c0), 2.0 ** 14, ALU.mult, ALU.mult))
                    v.sem_inc(w_scale, 1)

            v.wait_ge(norm_in, 32)
            link(v.tensor_reduce(col(peak, PQ), norm_b[:, 0:NH, :].rearrange("p h d -> p (h d)"), AX, ALU.max,
                                 apply_absolute_value=True))
            link(v.tensor_reduce(col(peak, PK), norm_b[:, NH:NQK, :].rearrange("p h d -> p (h d)"), AX,
                                 ALU.max, apply_absolute_value=True))
            powers(PQ, PK + 1)
            link(v.tensor_scalar(FQ, col(inv2, PQ), -2.0 ** 9, None, ALU.mult))
            link(v.tensor_scalar(FK, col(inv2, PK), 2.0 ** 10, None, ALU.mult))
            link(v.tensor_scalar(FS, col(pow2, PQ), col(pow2, PK), 2.0 ** -19 * float(HD) ** -0.5,
                                 ALU.mult, ALU.mult))
            v.wait_ge(angles_in, 32)
            link(v.tensor_tensor(rope_c[:], norm_b, cos_sb[:].unsqueeze(1).broadcast_to([P, NQK, HD]),
                                 ALU.mult))
            link(v.tensor_tensor(halves(rope_s[:]), rot(norm_b),
                                 sin_sb[:].rearrange("p (o two e) -> p o two e", o=1, two=2)
                                 .broadcast_to([P, NQK, 2, HD // 2]), ALU.mult))
            for table in (rope_c, rope_s):
                link(v.tensor_scalar(table[:, 0:NH, :], table[:, 0:NH, :], FQ, None, ALU.mult))
                link(v.tensor_scalar(table[:, NH:NQK, :], table[:, NH:NQK, :], FK, None, ALU.mult))
            for i in range(3 * TILES + KT + 4):
                early_steps(i, step)
                for n in range(5):
                    if i == LOOK_AT[n]:
                        look_over(n)
                for n in range(5):
                    if i == SCALE_AT[n]:
                        make_scalings(n)
                if i < 3 * TILES:
                    v.wait_ge(w_y, i + 1)
                    if i >= 3:
                        wait_q(v, i - 3)
                    v.tensor_scalar(wem[i % 3].bitcast(U32), wy[i % 4].bitcast(U32), EXPONENT, None, ALU.bitwise_and
                                    ).then_inc(w_e, 1)
                if 0 < i <= 3 * TILES:
                    y, em_ = wy[(i - 1) % 4], wem[(i - 1) % 3]
                    v.wait_ge(w_em, i)
                    v.tensor_tensor(y, y, em_, ALU.add).then_inc(w_z, 1)
                t = i - 4
                if t >= 0:
                    v.wait_ge(w_hi, t + 1)
                    src = square_banks[t % 4][:].rearrange("p (k r) -> p k r", k=4)
                    dst, scale = weight_slot(t)
                    v.scalar_tensor_tensor(dst(1), src, scale, dst(0), ALU.mult, ALU.subtract).then_inc(w_lo, 1)
                if 0 < i <= 3 * TILES and not on_pool(i - 1):
                    v.wait_ge(w_z, i)
                    v.tensor_tensor(y, y, em_, ALU.subtract).then_inc(w_q, 1)
            v.wait_ge(w_lo, 3 * TILES + KT)
            v.sem_inc(setup_done, 1)

            drive(v, step)


_INS = ['x', 'ctx_512', 'L0_xattn_q_norm_w', 'L0_xattn_k_norm_w', 'L0_xattn_w_out', 'L0_ffn_gate_w', 'L0_ffn_up_w',
        'L0_ffn_down_w']


def kernel(**inputs):
    import numpy as _np
    import concourse.bacc as _bacc
    from concourse import mybir as _mybir
    from concourse.bass_utils import run_bass_kernel_spmd as _run

    nc = _bacc.Bacc("TRN2", target_bir_lowering=False, num_devices=1)
    arrays, args = {}, []

    def give(name, a):
        arrays[f"in_{name}_dram"] = a
        args.append(nc.dram_tensor(f"in_{name}_dram", a.shape, _mybir.dt.from_np(a.dtype), kind="ExternalInput").ap())

    for name in _INS:
        give(name, _np.ascontiguousarray(inputs[name]))
    shape = inputs['x'].shape
    tokens, head = shape[1], 32
    inv_freq = (1.0 / _np.float32(10000.0) ** (_np.arange(0, head, 2, dtype=_np.float32) / _np.float32(head))
                ).astype(_np.float32)
    freqs = _np.outer(_np.arange(tokens, dtype=_np.float32), inv_freq).astype(_np.float32)
    give('rope_cos', _np.concatenate([_np.cos(freqs), _np.cos(freqs)], -1).astype(_np.float32))
    give('rope_sin', _np.concatenate([-_np.sin(freqs), _np.sin(freqs)], -1).astype(_np.float32))
    give('causal', _np.where(_np.tril(_np.ones((tokens, tokens), bool)), 0.0, -1e30).astype(_np.float32))
    give('eye32', _np.eye(128, dtype=_np.float32))
    give('eye16', _np.eye(128, dtype=_np.float16))
    out = nc.dram_tensor("out_0_dram", shape, _mybir.dt.float32, kind="ExternalOutput").ap()
    bass_xattn_ffn(nc, *args, out)
    r = _run(nc, [arrays], core_ids=[0])
    return r.results[0]["out_0_dram"]
```
